# Optimizing a Trainium2 kernel written in Bass

```python
import numpy as np
import jax
import jax.numpy as jnp

def _softmax(x, axis=-1):
    return jax.nn.softmax(x, axis=axis)

def _gelu(x):
    return jax.nn.gelu(x, approximate=True)

def _silu(x):
    return jax.nn.silu(x)

def _sigmoid(x):
    return jax.nn.sigmoid(x)

def _layernorm(x, axis=-1, eps=1e-05):
    m = jnp.mean(x, axis=axis, keepdims=True)
    v = jnp.var(x, axis=axis, keepdims=True)
    return (x - m) / jnp.sqrt(v + eps)

def _scatter_add(tgt, idx, src, axis=0):
    return tgt.at[idx].add(src)

def _segment_sum(src, seg, n):
    return jax.ops.segment_sum(src, seg, n)
kernel_name = 'mk_seq_postln_d1_jaxref_r4_fa5f1f'

def setup_inputs(seed: int=0):
    np.random.seed(seed)
    _w = jnp.asarray

    def _L0_attn_setup():
        import jax, jax.numpy as jnp
        import numpy as np
        D_MODEL = 256
        N_HEADS = 16
        D_LATENT = 64
        HEAD_DIM = D_MODEL // N_HEADS

        def apply_rope(x):
            B, T, H, D = x.shape
            inv_freq = 1.0 / 10000.0 ** (jnp.arange(0, D, 2, dtype=jnp.float32) / D)
            t = jnp.arange(T, dtype=jnp.float32)
            freqs = t[:, None] * inv_freq[None, :]
            sin_f = jnp.sin(freqs)[None, :, None, :]
            cos_f = jnp.cos(freqs)[None, :, None, :]
            x1, x2 = jnp.split(x, 2, axis=-1)
            return jnp.concatenate([x1 * cos_f - x2 * sin_f, x1 * sin_f + x2 * cos_f], axis=-1)
        key = jax.random.key(seed)
        ks = jax.random.split(key, 10)
        B, T = (4, 1024)
        s = lambda fan_in: 1.0 / np.sqrt(fan_in)
        return {'x': jax.random.normal(ks[0], (B, T, D_MODEL), dtype=jnp.float32), 'Wq': jax.random.normal(ks[1], (D_MODEL, D_MODEL), dtype=jnp.float32) * s(D_MODEL), 'bq': jnp.zeros((D_MODEL,), jnp.float32), 'Wdown': jax.random.normal(ks[2], (D_MODEL, D_LATENT), dtype=jnp.float32) * s(D_MODEL), 'bdown': jnp.zeros((D_LATENT,), jnp.float32), 'Wup': jax.random.normal(ks[3], (D_LATENT, 2 * D_MODEL), dtype=jnp.float32) * s(D_LATENT), 'bup': jnp.zeros((2 * D_MODEL,), jnp.float32), 'Wout': jax.random.normal(ks[4], (D_MODEL, D_MODEL), dtype=jnp.float32) * s(D_MODEL), 'bout': jnp.zeros((D_MODEL,), jnp.float32)}
    _L0_attn_in = _L0_attn_setup()

    def _L0_ffn_setup():
        import jax, jax.numpy as jnp
        import numpy as np
        CAPACITY_FACTOR = 0.5
        key = jax.random.key(seed)
        ks = jax.random.split(key, 5)
        B, S, D, F = (4, 1024, 256, 1024)
        scale_in = 1.0 / np.sqrt(D)
        scale_ff = 1.0 / np.sqrt(F)
        return {'hidden_states': jax.random.normal(ks[0], (B, S, D), dtype=jnp.float32), 'w_router': jax.random.normal(ks[1], (D,), dtype=jnp.float32) * scale_in, 'W1': jax.random.normal(ks[2], (D, F), dtype=jnp.float32) * scale_in, 'b1': jnp.zeros((F,), dtype=jnp.float32), 'W2': jax.random.normal(ks[3], (F, D), dtype=jnp.float32) * scale_ff, 'b2': jnp.zeros((D,), dtype=jnp.float32)}
    _L0_ffn_in = _L0_ffn_setup()
    _d = {'L0_attn_x': _L0_attn_in['x'], 'L0_attn_Wq': _L0_attn_in['Wq'], 'L0_attn_bq': _L0_attn_in['bq'], 'L0_attn_Wdown': _L0_attn_in['Wdown'], 'L0_attn_bdown': _L0_attn_in['bdown'], 'L0_attn_Wup': _L0_attn_in['Wup'], 'L0_attn_bup': _L0_attn_in['bup'], 'L0_attn_Wout': _L0_attn_in['Wout'], 'L0_attn_bout': _L0_attn_in['bout'], 'L0_ffn_w_router': _L0_ffn_in['w_router'], 'L0_ffn_W1': _L0_ffn_in['W1'], 'L0_ffn_b1': _L0_ffn_in['b1'], 'L0_ffn_W2': _L0_ffn_in['W2'], 'L0_ffn_b2': _L0_ffn_in['b2']}
    _x0 = _d['L0_attn_x']
    _d['L0_attn_x'] = jax.random.normal(jax.random.fold_in(jax.random.key(seed), 1), (8, 1024, 256), dtype=_x0.dtype)
    del _x0
    return _d

def reference(L0_attn_x, L0_attn_Wq, L0_attn_bq, L0_attn_Wdown, L0_attn_bdown, L0_attn_Wup, L0_attn_bup, L0_attn_Wout, L0_attn_bout, L0_ffn_w_router, L0_ffn_W1, L0_ffn_b1, L0_ffn_W2, L0_ffn_b2):

    def _L0_attn_ref(x, Wq, bq, Wdown, bdown, Wup, bup, Wout, bout):
        import jax, jax.numpy as jnp
        import numpy as np
        D_MODEL = 256
        N_HEADS = 16
        D_LATENT = 64
        HEAD_DIM = D_MODEL // N_HEADS

        def apply_rope(x):
            B, T, H, D = x.shape
            inv_freq = 1.0 / 10000.0 ** (jnp.arange(0, D, 2, dtype=jnp.float32) / D)
            t = jnp.arange(T, dtype=jnp.float32)
            freqs = t[:, None] * inv_freq[None, :]
            sin_f = jnp.sin(freqs)[None, :, None, :]
            cos_f = jnp.cos(freqs)[None, :, None, :]
            x1, x2 = jnp.split(x, 2, axis=-1)
            return jnp.concatenate([x1 * cos_f - x2 * sin_f, x1 * sin_f + x2 * cos_f], axis=-1)
        B, T, D = x.shape
        H, Dh = (N_HEADS, HEAD_DIM)
        q = x @ Wq + bq
        kv_latent = x @ Wdown + bdown
        kv = kv_latent @ Wup + bup
        q = q.reshape(B, T, H, Dh)
        kv = kv.reshape(B, T, H, 2 * Dh)
        k, v = jnp.split(kv, 2, axis=-1)
        q = apply_rope(q)
        k = apply_rope(k)
        att = jnp.einsum('bthd,btgd->bthg', q, k) / jnp.sqrt(jnp.float32(Dh))
        att = jax.nn.softmax(att, axis=-1)
        out = jnp.einsum('bthg,btgd->bthd', att, v)
        out = out.reshape(B, T, D)
        return out @ Wout + bout

    def _L0_ffn_ref(hidden_states, w_router, W1, b1, W2, b2):
        import jax, jax.numpy as jnp
        import numpy as np
        CAPACITY_FACTOR = 0.5
        'Mixture-of-Depths block: route top-k tokens through an FFN inner block,\n            scatter back with sigmoid router weights; bypassed tokens pass through.'
        B, S, D = hidden_states.shape
        k = int(S * CAPACITY_FACTOR)
        scores = jnp.einsum('bsd,d->bs', hidden_states, w_router)
        top_scores, top_idx = jax.lax.top_k(scores, k)
        weights = jax.nn.sigmoid(top_scores)
        selected = jnp.take_along_axis(hidden_states, top_idx[:, :, None], axis=1)
        h = jax.nn.gelu(jnp.einsum('bkd,df->bkf', selected, W1) + b1)
        processed = jnp.einsum('bkf,fd->bkd', h, W2) + b2
        update = weights[:, :, None] * processed

        def scatter_one(xb, ib, ub):
            return xb.at[ib].add(ub)
        output = jax.vmap(scatter_one)(hidden_states, top_idx, update)
        return output
    x = L0_attn_x
    x = _layernorm(x + _L0_attn_ref(x, L0_attn_Wq, L0_attn_bq, L0_attn_Wdown, L0_attn_bdown, L0_attn_Wup, L0_attn_bup, L0_attn_Wout, L0_attn_bout), axis=-1)
    x = _layernorm(x + _L0_ffn_ref(x, L0_ffn_w_router, L0_ffn_W1, L0_ffn_b1, L0_ffn_W2, L0_ffn_b2), axis=-1)
    return x

_drawn_inputs = setup_inputs


def setup_inputs(seed=0):
    import zlib

    import numpy as np

    out = dict(_drawn_inputs(seed))
    spreads = {'L0_attn_bq': (0.0, 0.1),
     'L0_attn_bdown': (0.0, 0.1),
     'L0_attn_bup': (0.0, 0.1),
     'L0_attn_bout': (0.0, 0.1),
     'L0_ffn_b1': (0.0, 0.517),
     'L0_ffn_b2': (0.0, 0.354)}
    factors = {}
    for name, (base, spread) in spreads.items():
        noise = np.random.default_rng([zlib.crc32(name.encode()), seed]).standard_normal(out[name].shape)
        drawn = base * np.exp(spread * noise) if base else spread * noise
        out[name] = jnp.asarray(drawn.astype(out[name].dtype))
    for name, factor in factors.items():
        out[name] = (out[name] * factor).astype(out[name].dtype)
    return out
```

```python
from contextlib import ExitStack

import concourse.bass as bass
from concourse import mybir

F32 = mybir.dt.float32
U32 = mybir.dt.uint32
I32 = mybir.dt.int32
ALU = mybir.AluOpType
ACT = mybir.ActivationFunctionType
AX = mybir.AxisListType

P = 128
EPS = 1e-5


def build_layer(nc, xT, x, Wq, bq, Wdown, bdown, Wup, Wout, bout, w_router, W1, b1, W2, b2, out,
                x1_dram, score_dram, perm_dram, proc_dram):
    N, D = out.shape
    H, DH = 16, D // 16
    L = Wdown.shape[1]
    F = W1.shape[1]
    S = 1024
    B = N // S
    TB = S // P
    K = S // 2
    SB_ = K // P
    KD = D // P
    FT = F // P
    PAIRS = H * H * DH
    ZROW = B * K
    TILES = B * TB
    QH_POOL = 10
    PG_POOL = 10
    SCALE = float(DH) ** -0.5

    with ExitStack() as ctx:
        def sb(name, shape, dt=F32):
            return ctx.enter_context(nc.sbuf_tensor(name, shape, dt))

        def ps(name):
            return ctx.enter_context(nc.psum_tensor(name, [P, 512], F32))

        def sem(name):
            return ctx.enter_context(nc.semaphore(name))

        wq_sb = sb("wq_sb", [P, KD, D])
        wdown_sb = sb("wdown_sb", [P, KD, L])
        wup_sb = sb("wup_sb", [L + 1, 2 * D])
        wout_sb = sb("wout_sb", [P, KD, D])
        w1_sb = sb("w1_sb", [P, KD, F])
        w2_sb = sb("w2_sb", [P, FT, D])
        bq_sb = sb("bq_sb", [1, D])
        bout_sb = sb("bout_sb", [1, D])
        bdown_sb = sb("bdown_sb", [L, 1])
        b1_sb = sb("b1_sb", [P, FT])
        b2_sb = sb("b2_sb", [P, D])
        router_sb = sb("router_sb", [P, D])
        ident = sb("ident", [P, P])
        before = sb("before", [P, P])
        ones_row = sb("ones_row", [1, P])
        minus_half = sb("minus_half", [P, 2])
        zero_rows = sb("zero_rows", [P, 8 * D])

        xT_sb = sb("xT_sb", [P, 4, KD, P])
        x_sb = sb("x_sb", [P, 4, D])
        latT_sb = sb("latT_sb", [L + 1, P])
        q_sb = sb("q_sb", [P, 2, D])
        kv_sb = sb("kv_sb", [P, 2, 2 * D])
        qk_prod = sb("qk_prod", [P, 2, PAIRS])
        logits = sb("logits", [P, H * H])
        row_max = sb("row_max", [P, H])
        expo = sb("expo", [P, H * H])
        row_sum = sb("row_sum", [P, H])
        row_inv = sb("row_inv", [P, H])
        probs = sb("probs", [P, 2, H * H])
        pv_prod = sb("pv_prod", [P, 2, PAIRS])
        oT_sb = sb("oT_sb", [P, 2, P])
        resid = sb("resid", [P, D])
        stats = sb("stats", [P, 2, 6])
        mean_var = sb("mean_var", [P, 2, 2])
        var_eps = sb("var_eps", [P, 2])
        rstd = sb("rstd", [P, 2])
        x1_sb = sb("x1_sb", [P, 4, D])
        score_junk = sb("score_junk", [P, D])

        score_new = sb("score_new", [P, TB])
        score_old = sb("score_old", [P, TB])
        score_row = sb("score_row", [P, S])
        rank_junk = sb("rank_junk", [P, S])
        counts = sb("counts", [P, 3, TB])
        rank_f = sb("rank_f", [P, TB])
        rank_u = sb("rank_u", [P, TB], U32)
        chosen = sb("chosen", [P, TB])
        route_f = sb("route_f", [P, TB])
        route = [sb(f"route{i}", [P, TB], U32) for i in range(3)]
        gate_exp = sb("gate_exp", [P, TB])
        gate = [sb(f"gate{i}", [P, TB]) for i in range(3)]
        slot_base = sb("slot_base", [P, 1])
        token_id = sb("token_id", [P, TB], U32)
        perm_sb = sb("perm_sb", [P, SB_], U32)
        chosen_x = sb("chosen_x", [P, SB_, D])
        chosenT = sb("chosenT", [P, KD, K])
        hidT = sb("hidT", [P, FT, K])
        proc_sb = sb("proc_sb", [P, 2, D])
        x1_back = sb("x1_back", [P, 2, D])
        upd = sb("upd", [P, 2, D])
        upd_gated = sb("upd_gated", [P, D])
        z_sb = sb("z_sb", [P, D])
        out_sb = sb("out_sb", [P, 2, D])

        psQ, psKV, psO0, psO1, psW, psF0, psF1, psP = [ps(n) for n in
            ("psQ", "psKV", "psO0", "psO1", "psW", "psF0", "psF1", "psP")]
        psO, psF = [psO0, psO1], [psF0, psF1]

        weights_loaded = sem("weights_loaded")
        xT_loaded = [sem(f"xT_loaded{i}") for i in range(4)]
        x_loaded = [sem(f"x_loaded{i}") for i in range(4)]
        x1_stored = [sem(f"x1_stored{i}") for i in range(4)]
        score_stored, row_loaded, perm_loaded = sem("score_stored"), sem("row_loaded"), sem("perm_loaded")
        zero_stored = sem("zero_stored")
        proc_stored = [sem(f"proc_stored{i}") for i in range(2)]
        x1_back_loaded = [sem(f"x1_back_loaded{i}") for i in range(2)]
        out_stored = [sem(f"out_stored{i}") for i in range(2)]
        perm_scattered, chosen_gathered = sem("perm_scattered"), sem("chosen_gathered")
        upd_gathered = [sem(f"upd_gathered{i}") for i in range(2)]
        passed = {"DVE": sem("dve_passed"), "Pool": sem("pool_passed"), "SP": sem("sp_passed")}
        pool_cleared, consts_ready, dve_consts = sem("pool_cleared"), sem("consts_ready"), sem("dve_consts")
        lat_made, lat_copied = sem("lat_made"), sem("lat_copied")
        q_made, q_copied, kv_made, kv_copied = sem("q_made"), sem("q_copied"), sem("kv_made"), sem("kv_copied")
        qk_pool, qk_dve, logits_dve, logits_ready = sem("qk_pool"), sem("qk_dve"), sem("logits_dve"), sem("logits_ready")
        max_ready, shifted, exp_ready = sem("max_ready"), sem("shifted"), sem("exp_ready")
        sum_ready, inv_ready, probs_ready = sem("sum_ready"), sem("inv_ready"), sem("probs_ready")
        pv_pool, pv_dve, oT_made, oT_copied = sem("pv_pool"), sem("pv_dve"), sem("oT_made"), sem("oT_copied")
        attn_made, resid_ready, stats_ready = sem("attn_made"), sem("resid_ready"), sem("stats_ready")
        mv_ready, var_ready, rstd_ready = sem("mv_ready"), sem("var_ready"), sem("rstd_ready")
        x1_ready, score_ready = sem("x1_ready"), sem("score_ready")
        gated_ready, z_ready, zstats_ready = sem("gated_ready"), sem("z_ready"), sem("zstats_ready")
        zmv_ready, zvar_ready, out_ready = sem("zmv_ready"), sem("zvar_ready"), sem("out_ready")
        score_kept, counted = sem("score_kept"), sem("counted")
        rank_step, routed, shifted_route, gate_exped = sem("rank_step"), sem("routed"), sem("shifted_route"), sem("gate_exped")
        chosenT_made, chosenT_copied = sem("chosenT_made"), sem("chosenT_copied")
        hid_made, hid_ready, proc_made, proc_ready = sem("hid_made"), sem("hid_ready"), sem("proc_made"), sem("proc_ready")

        def wait(eng, s, value):
            if not (isinstance(value, int) and value <= 0):
                eng.wait_ge(s, value)

        def wait_alone(eng, s, value):
            wait(eng, s, value)
            if not isinstance(value, int):
                eng.sem_inc(passed[eng.engine.name], 1)

        N_WEIGHTS = 12
        N_ZERO = 1 + N // S + B * K // S

        def parts(T):
            steady = not isinstance(T, int)
            return dict(
                attn=steady or T < TILES, mix=steady or 1 <= T <= TILES, norm=steady or 2 <= T <= TILES + 1,
                rank=steady or TB <= T < TILES + TB, ffn=steady or 2 * TB <= T < TILES + 2 * TB,
                last=steady or 3 * TB <= T < TILES + 3 * TB)

        def program(eng, step):
            for b in range(4):
                for t in range(TB):
                    step(b, t)
            with eng.Fori(4, B) as b:
                for t in range(TB):
                    step(b, t)
            for b in range(B, B + 3):
                for t in range(TB):
                    step(b, t)

        block = ctx.enter_context(nc.Block())

        @block.sync
        def _(sp):
            def load_x(T, b, t):
                wait_alone(sp, resid_ready, T - 3)
                sp.dma_start(x_sb[:, t % 4, :], x[bass.ds(T * P, P), :]).then_inc(x_loaded[t % 4], 16)

            def load_xT(T, b, t):
                wait_alone(sp, q_made, T - 3)
                wait_alone(sp, lat_made, T - 3)
                sp.dma_start(xT_sb[:, t % 4, :, :], xT[bass.ds(T * P, P), :].rearrange("k (a n) -> k a n", a=KD)
                             ).then_inc(xT_loaded[t % 4], 16)

            sp.dma_start(wdown_sb[:], Wdown.rearrange("(a k) n -> k a n", a=KD)).then_inc(weights_loaded, 16)
            sp.dma_start(wq_sb[:], Wq.rearrange("(a k) n -> k a n", a=KD)).then_inc(weights_loaded, 16)
            sp.dma_start(bdown_sb[:], bdown).then_inc(weights_loaded, 16)
            sp.dma_start(bq_sb[:], bq).then_inc(weights_loaded, 16)
            sp.dma_start(wup_sb[:], Wup).then_inc(weights_loaded, 16)
            load_xT(0, 0, 0)
            load_xT(1, 0, 1)
            load_x(0, 0, 0)
            sp.dma_start(wout_sb[:], Wout.rearrange("(a k) n -> k a n", a=KD)).then_inc(weights_loaded, 16)
            sp.dma_start(bout_sb[:], bout).then_inc(weights_loaded, 16)
            sp.dma_start(router_sb[:], w_router.broadcast_to([P, D])).then_inc(weights_loaded, 16)
            sp.dma_start(w1_sb[:], W1.rearrange("(a k) n -> k a n", a=KD)).then_inc(weights_loaded, 16)
            sp.dma_start(b1_sb[:], b1).then_inc(weights_loaded, 16)
            sp.dma_start(w2_sb[:], W2.rearrange("(a k) n -> k a n", a=FT)).then_inc(weights_loaded, 16)
            sp.dma_start(b2_sb[:], b2.broadcast_to([P, D])).then_inc(weights_loaded, 16)
            sp.wait_ge(dve_consts, 1)
            sp.dma_start(proc_dram[ZROW:ZROW + 1, :], zero_rows[0:1, 0:D]).then_inc(zero_stored, 16)
            for n in range(N // S):
                sp.dma_start(x1_dram[n * S:(n + 1) * S, :].rearrange("(p a) d -> p (a d)", p=P), zero_rows[:]
                             ).then_inc(zero_stored, 16)
            for n in range(B * K // S):
                sp.dma_start(proc_dram[n * S:(n + 1) * S, :].rearrange("(p a) d -> p (a d)", p=P), zero_rows[:]
                             ).then_inc(zero_stored, 16)
            sp.wait_ge(zero_stored, N_ZERO * 16)

            def step(b, t):
                T = b * TB + t
                on = parts(T)
                if on["attn"]:
                    load_xT(T + 2, b, t + 2)
                    load_x(T + 1, b, t + 1)
                if on["last"]:
                    f = T - 3 * TB
                    wait_alone(sp, z_ready, f - 1)
                    sp.dma_start(x1_back[:, t % 2, :], x1_dram[bass.ds(f * P, P), :]
                                 ).then_inc(x1_back_loaded[t % 2], 16)
                if on["norm"]:
                    i = T - 2
                    wait_alone(sp, x1_ready, i + 1)
                    sp.dma_start(x1_dram[bass.ds(i * P, P), :], x1_sb[:, (t + 2) % 4, :]
                                 ).then_inc(x1_stored[(t + 2) % 4], 16)
                if on["rank"] and t == 1:
                    wait_alone(sp, score_kept, b)
                    sp.dma_start(score_dram.rearrange("a (t p) -> (a p) t", p=P), score_old[:],
                                 allow_slow_non_contiguous=True).then_inc(score_stored, 16)
                    wait_alone(sp, score_stored, 16 * b)
                    wait_alone(sp, counted, 3 * TB * (b - 1))
                    sp.dma_start(score_row[:], score_dram.broadcast_to([P, S])).then_inc(row_loaded, 16)
                if on["rank"] and t == 6:
                    wait_alone(sp, perm_scattered, 16 * TB * b)
                    wait_alone(sp, chosen_gathered, 16 * SB_ * (b - 1))
                    sp.dma_start(perm_sb[:], perm_dram[0:K, :].rearrange("(s p) a -> p (s a)", p=P),
                                 allow_slow_non_contiguous=True).then_inc(perm_loaded, 16)
                if on["ffn"] and t >= 4:
                    n = (b - 2) * SB_ + t - 4
                    wait_alone(sp, proc_ready, n + 1)
                    sp.dma_start(proc_dram[bass.ds(n * P, P), :], proc_sb[:, t % 2, :]
                                 ).then_inc(proc_stored[t % 2], 16)
                if on["last"]:
                    f = T - 3 * TB
                    wait_alone(sp, out_ready, f + 1)
                    sp.dma_start(out[bass.ds(f * P, P), :], out_sb[:, t % 2, :]).then_inc(out_stored[t % 2], 16)

            program(sp, step)
            for i in range(2):
                sp.wait_ge(out_stored[i], 16 * TILES // 2)
                sp.wait_ge(proc_stored[i], 16 * B * SB_ // 2)
            for i in range(4):
                sp.wait_ge(x1_stored[i], 16 * TILES // 4)
            for i in range(2):
                sp.wait_ge(xT_loaded[i], 16 * (TILES // 4 + 1))
            sp.wait_ge(x_loaded[0], 16 * (TILES // 4 + 1))

        @block.tensor
        def _(pe):
            def step(b, t):
                T = b * TB + t
                on = parts(T)
                if on["attn"]:
                    u = t % 4
                    wait(pe, xT_loaded[u], 16 * (2 * b + t // 4 + 1))
                    wait(pe, kv_copied, T)
                    for a in range(KD):
                        mm = pe.matmul(psKV[0:L, 0:P], wdown_sb[:, a, :], xT_sb[:, u, a, :],
                                       start=(a == 0), stop=(a == KD - 1))
                    mm.then_inc(lat_made, 1)
                    wait(pe, q_copied, T)
                    pe.matmul(psQ[:, 0:D], ones_row[:], bq_sb[:], start=True, stop=False)
                    for a in range(KD):
                        mm = pe.matmul(psQ[:, 0:D], xT_sb[:, u, a, :], wq_sb[:, a, :],
                                       start=False, stop=(a == KD - 1))
                    mm.then_inc(q_made, 1)
                    wait(pe, lat_copied, T + 1)
                    pe.matmul(psKV[:], latT_sb[:], wup_sb[:], start=True, stop=True).then_inc(kv_made, 1)
                if on["norm"]:
                    i = T - 2
                    wait(pe, oT_copied, i + 1)
                    wait(pe, resid_ready, i)
                    pe.matmul(psW[:, 0:D], ones_row[:], bout_sb[:], start=True, stop=False)
                    for a in range(KD):
                        mm = pe.matmul(psW[:, 0:D], oT_sb[:, a, :], wout_sb[:, a, :],
                                       start=False, stop=(a == KD - 1))
                    mm.then_inc(attn_made, 1)
                if on["ffn"] and t < 4:
                    for f in (2 * t, 2 * t + 1):
                        n = (b - 2) * FT + f
                        wait(pe, hid_ready, n - 1)
                        if f < 2:
                            wait(pe, chosenT_copied, 2 * (b - 1))
                        for a in range(KD):
                            mm = pe.matmul(psF[f % 2][:], w1_sb[:, a, f * P:(f + 1) * P], chosenT[:, a, :],
                                           start=(a == 0), stop=(a == KD - 1))
                        mm.then_inc(hid_made, 1)
                if on["ffn"] and t >= 4:
                    s = t - 4
                    n = (b - 2) * SB_ + s
                    wait(pe, hid_ready, (b - 1) * FT)
                    wait(pe, proc_ready, n)
                    for f in range(FT):
                        mm = pe.matmul(psP[:, 0:D], hidT[:, f, s * P:(s + 1) * P], w2_sb[:, f, :],
                                       start=(f == 0), stop=(f == FT - 1))
                    mm.then_inc(proc_made, 1)
                if on["mix"]:
                    i = T - 1
                    u = (t + 1) % 2
                    wait(pe, oT_copied, i)
                    for half in range(2):
                        order = list(range(PG_POOL, H)) + list(range(PG_POOL))
                        for n, g in enumerate(order):
                            if half == 0 and n == 0:
                                wait(pe, pv_dve, i + 1)
                            if half == 0 and g == 0:
                                wait(pe, pv_pool, i + 1)
                            mm = pe.matmul(psO[half][:, 0:P],
                                           pv_prod[:, u, g * D + half * P:g * D + (half + 1) * P], ident[:],
                                           start=(n == 0), stop=(n == H - 1), is_transpose=True)
                    mm.then_inc(oT_made, 1)
                if on["rank"] and t == 7:
                    wait(pe, chosen_gathered, 16 * SB_ * b)
                    wait(pe, hid_ready, (b - 1) * FT)
                    for a in range(KD):
                        for s in range(SB_):
                            mm = pe.transpose(psF[a][:, s * P:(s + 1) * P], chosen_x[:, s, a * P:(a + 1) * P], ident[:])
                        mm.then_inc(chosenT_made, 1)

            pe.wait_ge(weights_loaded, 16 * N_WEIGHTS)
            pe.wait_ge(consts_ready, 1)
            pe.wait_ge(dve_consts, 1)
            program(pe, step)

        @block.scalar
        def _(act):
            def step(b, t):
                T = b * TB + t
                on = parts(T)
                if on["attn"]:
                    wait(act, lat_made, T + 1)
                    wait(act, kv_made, T)
                    nc.scalar.activation(latT_sb[0:L, :], psKV[0:L, 0:P], ACT.Identity, bias=bdown_sb[:]
                                         ).then_inc(lat_copied, 1)
                    wait(act, q_made, T + 1)
                    wait(act, qk_dve, T - 1)
                    wait(act, qk_pool, T - 1)
                    nc.scalar.activation(q_sb[:, t % 2, :], psQ[:, 0:D], ACT.Copy, scale=SCALE).then_inc(q_copied, 1)
                    wait(act, kv_made, T + 1)
                    wait(act, pv_dve, T - 1)
                    wait(act, pv_pool, T - 1)
                    nc.scalar.activation(kv_sb[:, t % 2, :], psKV[:], ACT.Copy).then_inc(kv_copied, 1)
                if on["rank"] and t == 2:
                    wait(act, score_kept, b)
                    wait(act, routed, b - 1)
                    nc.scalar.activation(gate_exp[:], score_old[:], ACT.Exp, scale=-1.0).then_inc(gate_exped, 1)
                if on["last"]:
                    f = T - 3 * TB
                    wait(act, upd_gathered[t % 2], 16 * ((b - 3) * (TB // 2) + t // 2 + 1))
                    wait(act, shifted_route, 2 * (b - 1))
                    wait(act, z_ready, f)
                    nc.scalar.activation(upd_gated[:], upd[:, t % 2, :], ACT.Copy, scale=gate[2][:, t:t + 1]
                                         ).then_inc(gated_ready, 1)
                if on["attn"]:
                    wait(act, shifted, T + 1)
                    wait(act, probs_ready, T)
                    nc.scalar.activation(expo[:], logits[:], ACT.Exp).then_inc(exp_ready, 1)
                if on["mix"]:
                    i = T - 1
                    wait(act, oT_made, i + 1)
                    wait(act, attn_made, i)
                    nc.scalar.activation(oT_sb[:, 0, :], psO0[:, 0:P], ACT.Copy)
                    nc.scalar.activation(oT_sb[:, 1, :], psO1[:, 0:P], ACT.Copy).then_inc(oT_copied, 1)
                if on["ffn"] and t < 4:
                    for f in (2 * t, 2 * t + 1):
                        n = (b - 2) * FT + f
                        wait(act, hid_made, n + 1)
                        wait(act, proc_made, (b - 2) * SB_)
                        nc.scalar.activation(hidT[:, f, :], psF[f % 2][:], ACT.Gelu_apprx_tanh,
                                             bias=b1_sb[:, f:f + 1]).then_inc(hid_ready, 1)
                if on["rank"] and t == 7:
                    for a in range(KD):
                        wait(act, chosenT_made, 2 * (b - 1) + a + 1)
                        wait(act, hid_made, (b - 1) * FT)
                        nc.scalar.activation(chosenT[:, a, :], psF[a][:], ACT.Copy).then_inc(chosenT_copied, 1)

            act.wait_ge(weights_loaded, 16 * N_WEIGHTS)
            program(act, step)

        def heads(ap, h0, h1):
            return ap.rearrange("p (h d) -> p h d", h=H)[:, h0:h1, :].unsqueeze(2).broadcast_to([P, h1 - h0, H, DH])

        def qk_products(eng, u, h0, h1):
            keys = kv_sb[:, u, :].rearrange("p (g e) -> p g e", g=H)[:, :, 0:DH]
            return eng.tensor_tensor(
                qk_prod[:, u, h0 * H * DH:h1 * H * DH].rearrange("p (h g d) -> p h g d", h=h1 - h0, g=H),
                heads(q_sb[:, u, :], h0, h1), keys.unsqueeze(1).broadcast_to([P, h1 - h0, H, DH]), ALU.mult)

        def pv_products(eng, u, g0, g1):
            weight = probs[:, u, :].rearrange("p (h g) -> p g h", h=H)[:, g0:g1, :]
            values = kv_sb[:, u, :].rearrange("p (g e) -> p g e", g=H)[:, g0:g1, DH:2 * DH]
            return eng.tensor_tensor(
                pv_prod[:, u, g0 * H * DH:g1 * H * DH].rearrange("p (g h d) -> p g h d", g=g1 - g0, h=H),
                weight.unsqueeze(3).broadcast_to([P, g1 - g0, H, DH]),
                values.unsqueeze(2).broadcast_to([P, g1 - g0, H, DH]), ALU.mult)

        @block.gpsimd
        def _(pool):
            pool.memset(ident[:], 0.0).then_inc(pool_cleared, 1)
            pool.memset(before[:], 1.0).then_inc(pool_cleared, 1)
            pool.iota(token_id[:].bitcast(I32), [[P, TB]], base=0, channel_multiplier=1).then_inc(pool_cleared, 1)
            pool.wait_ge(pool_cleared, 3)
            pool.affine_select(out=ident[:], in_=ident[:], compare_op=ALU.not_equal, fill=1.0, base=0,
                               pattern=[[-1, P]], channel_multiplier=1).then_inc(pool_cleared, 1)
            pool.affine_select(out=before[:], in_=before[:], compare_op=ALU.is_gt, fill=0.0, base=0,
                               pattern=[[-1, P]], channel_multiplier=1).then_inc(pool_cleared, 1)
            pool.wait_ge(pool_cleared, 5)
            pool.memset(minus_half[:], -0.5).then_inc(consts_ready, 1)
            pool.wait_ge(dve_consts, 1)

            def step(b, t):
                T = b * TB + t
                on = parts(T)
                if on["last"]:
                    f = T - 3 * TB
                    if t == 0:
                        for i in range(2):
                            wait(pool, proc_stored[i], (b - 2) * (16 * SB_ // 2))
                        wait(pool, zero_stored, 16 * N_ZERO)
                        wait(pool, shifted_route, 2 * (b - 1))
                    wait_alone(pool, gated_ready, f - 1)
                    pool.indirect_dma_start(upd[:, t % 2, :], None, proc_dram,
                                            bass.IndirectOffsetOnAxis(route[2][:, t:t + 1], 0)
                                            ).then_inc(upd_gathered[t % 2], 16)
                if on["mix"]:
                    i = T - 1
                    u = (t + 1) % 2
                    wait(pool, probs_ready, i + 1)
                    wait(pool, oT_made, i - 1)
                    pv_products(pool, u, 0, PG_POOL).then_inc(pv_pool, 1)
                if on["attn"]:
                    u = t % 2
                    wait(pool, q_copied, T + 1)
                    wait(pool, kv_copied, T + 1)
                    wait(pool, logits_ready, T - 1)
                    qk_products(pool, u, 0, QH_POOL).then_inc(qk_pool, 1)
                if on["norm"] or on["last"]:
                    if on["norm"]:
                        wait(pool, var_ready, T - 1)
                    if on["last"]:
                        wait(pool, zvar_ready, T - 3 * TB + 1)
                        wait(pool, out_ready, T - 3 * TB)
                    wait(pool, x1_ready, T - 2 if on["norm"] else TILES)
                    pool.tensor_tensor(rstd[:], var_eps[:], minus_half[:], ALU.pow).then_inc(rstd_ready, 1)
                if on["rank"] and t == 5:
                    wait(pool, perm_loaded, 16 * (b - 1))
                    wait_alone(pool, routed, b)
                    for n in range(TB):
                        pool.indirect_dma_start(perm_dram, bass.IndirectOffsetOnAxis(rank_u[:, n:n + 1], 0),
                                                token_id[:, n:n + 1], None).then_inc(perm_scattered, 16)
                if on["rank"] and t == 6:
                    for i in range(4):
                        wait(pool, x1_stored[i], 16 * TB // 4 * b)
                    wait(pool, chosenT_made, 2 * (b - 1))
                    wait_alone(pool, perm_loaded, 16 * b)
                    for s in range(SB_):
                        pool.indirect_dma_start(chosen_x[:, s, :], None, x1_dram,
                                                bass.IndirectOffsetOnAxis(perm_sb[:, s:s + 1], 0)
                                                ).then_inc(chosen_gathered, 16)

            program(pool, step)

        @block.vector
        def _(dve):
            dve.memset(latT_sb[L:L + 1, :], 1.0)
            dve.memset(ones_row[:], 1.0)
            dve.memset(counts[:], 0.0)
            dve.memset(var_eps[:], 1.0)
            dve.memset(slot_base[:], float(-ZROW))
            for i in range(3):
                dve.memset(gate[i][:], 0.0)
                dve.memset(route[i][:], 0)
            dve.memset(zero_rows[:], 0.0).then_inc(dve_consts, 1)
            dve.wait_ge(dve_consts, 1)
            dve.wait_ge(weights_loaded, 16 * N_WEIGHTS)
            dve.wait_ge(consts_ready, 1)

            def reduce_logits(u, h0, h1):
                return dve.tensor_reduce(
                    logits[:, h0 * H:h1 * H],
                    qk_prod[:, u, h0 * H * DH:h1 * H * DH].rearrange("p (n d) -> p n d", d=DH), AX.X, ALU.add)

            def step(b, t):
                T = b * TB + t
                on = parts(T)
                u = t % 2
                if t == 0 and (on["ffn"] or on["last"]):
                    wait(dve, out_ready, (b - 3) * TB)
                    for i in range(2):
                        wait(dve, upd_gathered[i], (b - 3) * (16 * TB // 2))
                    dve.tensor_copy(route[2][:], route[1][:])
                    dve.tensor_copy(gate[2][:], gate[1][:]).then_inc(shifted_route, 1)
                    dve.wait_ge(shifted_route, 2 * b - 3)
                    dve.tensor_copy(route[1][:], route[0][:])
                    dve.tensor_copy(gate[1][:], gate[0][:]).then_inc(shifted_route, 1)
                if t == 0 and on["rank"] and on["ffn"]:
                    wait(dve, perm_scattered, 16 * TB * (b - 1))
                    dve.tensor_scalar(token_id[:], token_id[:], float(S), None, ALU.add)
                    dve.tensor_scalar(slot_base[:], slot_base[:], float(K), None, ALU.add)
                if on["mix"]:
                    i = T - 1
                    wait(dve, probs_ready, i + 1)
                    wait(dve, oT_made, i - 1)
                    pv_products(dve, 1 - u, PG_POOL, H).then_inc(pv_dve, 1)
                if on["attn"]:
                    wait(dve, q_copied, T + 1)
                    wait(dve, kv_copied, T + 1)
                    wait(dve, logits_ready, T - 1)
                    qk_products(dve, u, QH_POOL, H).then_inc(qk_dve, 1)
                if on["norm"]:
                    i = T - 2
                    w = (t + 2) % 4
                    wait(dve, attn_made, i + 1)
                    wait(dve, x_loaded[w], 16 * (2 * b + (t - 2) // 4 + 1))
                    wait(dve, x1_ready, i)
                    dve.tensor_tensor(resid[:], psW[:, 0:D], x_sb[:, w, :], ALU.add).then_inc(resid_ready, 1)
                    wait(dve, resid_ready, i + 1)
                    dve.bn_stats(stats[:, 0, :], resid[:]).then_inc(stats_ready, 1)
                if on["attn"]:
                    wait(dve, qk_dve, T + 1)
                    wait(dve, exp_ready, T)
                    reduce_logits(u, QH_POOL, H).then_inc(logits_dve, 1)
                if on["norm"]:
                    i = T - 2
                    wait_alone(dve, stats_ready, i + 1)
                    dve.bn_aggr(mean_var[:, 0, :], stats[:, 0, :]).then_inc(mv_ready, 1)
                if on["last"]:
                    f = T - 3 * TB
                    wait(dve, gated_ready, f + 1)
                    wait(dve, x1_back_loaded[t % 2], 16 * ((b - 3) * (TB // 2) + t // 2 + 1))
                    wait(dve, out_ready, f)
                    dve.scalar_tensor_tensor(out=z_sb[:], in0=x1_back[:, t % 2, :], scalar=2.0, in1=upd_gated[:],
                                             op0=ALU.mult, op1=ALU.add).then_inc(z_ready, 1)
                if on["norm"]:
                    i = T - 2
                    wait(dve, mv_ready, i + 1)
                    wait(dve, rstd_ready, T - 2)
                    dve.tensor_scalar(var_eps[:, 0:1], mean_var[:, 0, 1:2], EPS, None, ALU.add).then_inc(var_ready, 1)
                if on["last"]:
                    wait(dve, z_ready, f + 1)
                    dve.bn_stats(stats[:, 1, :], z_sb[:]).then_inc(zstats_ready, 1)
                    wait_alone(dve, zstats_ready, f + 1)
                    dve.bn_aggr(mean_var[:, 1, :], stats[:, 1, :]).then_inc(zmv_ready, 1)
                    wait(dve, zmv_ready, f + 1)
                    wait(dve, rstd_ready, T - 2)
                    dve.tensor_scalar(var_eps[:, 1:2], mean_var[:, 1, 1:2], EPS, None, ALU.add).then_inc(zvar_ready, 1)
                if on["attn"]:
                    wait(dve, qk_pool, T + 1)
                    reduce_logits(u, 0, QH_POOL).then_inc(logits_ready, 1)
                    wait(dve, logits_dve, T + 1)
                    wait(dve, logits_ready, T + 1)
                    lg = logits[:].rearrange("p (h g) -> p h g", h=H)
                    dve.tensor_reduce(row_max[:], lg, AX.X, ALU.max).then_inc(max_ready, 1)
                    wait(dve, max_ready, T + 1)
                    dve.tensor_tensor(lg, lg, row_max[:].unsqueeze(2).broadcast_to([P, H, H]), ALU.subtract
                                      ).then_inc(shifted, 1)
                if on["norm"]:
                    i = T - 2
                    w = (t + 2) % 4
                    wait(dve, rstd_ready, T - 1)
                    wait(dve, x1_stored[w], 16 * (2 * b + (t - 2) // 4))
                    dve.tensor_scalar(x1_sb[:, w, :], resid[:], mean_var[:, 0, 0:1], rstd[:, 0:1],
                                      ALU.subtract, ALU.mult).then_inc(x1_ready, 1)
                    wait(dve, x1_ready, i + 1)
                    c = (t - 2) % TB
                    wait(dve, score_ready, i)
                    if t == 2:
                        wait(dve, score_kept, b)
                    dve.tensor_tensor_reduce(out=score_junk[:], in0=x1_sb[:, w, :], in1=router_sb[:], scale=1.0,
                                             scalar=0.0, op0=ALU.mult, op1=ALU.add,
                                             accum_out=score_new[:, c:c + 1]).then_inc(score_ready, 1)
                if on["last"]:
                    f = T - 3 * TB
                    wait(dve, rstd_ready, T - 1)
                    wait(dve, out_stored[t % 2], 16 * ((b - 3) * (TB // 2) + t // 2))
                    dve.tensor_scalar(out_sb[:, t % 2, :], z_sb[:], mean_var[:, 1, 0:1], rstd[:, 1:2],
                                      ALU.subtract, ALU.mult).then_inc(out_ready, 1)
                if on["rank"] and t == 1:
                    wait(dve, score_ready, TB * b)
                    wait(dve, score_stored, 16 * (b - 1))
                    wait(dve, gate_exped, b - 1)
                    wait(dve, counted, 3 * TB * (b - 1))
                    dve.tensor_copy(score_old[:], score_new[:]).then_inc(score_kept, 1)
                if on["rank"] and 2 <= t <= 5:
                    if t == 2:
                        wait(dve, row_loaded, 16 * b)
                        wait(dve, score_kept, b)
                    for n in (2 * t - 4, 2 * t - 3):
                        own = score_old[:, n:n + 1]
                        k = 3 * (TB * (b - 1) + n)
                        wait(dve, counted, k)
                        dve.tensor_scalar(rank_junk[:, n * P:S], score_row[:, n * P:S], own, None, ALU.is_gt,
                                          ALU.add, accum_out=counts[:, 0, n:n + 1]).then_inc(counted, 1)
                        wait(dve, counted, k + 1)
                        if n:
                            dve.tensor_scalar(rank_junk[:, 0:n * P], score_row[:, 0:n * P], own, None, ALU.is_ge,
                                              ALU.add, accum_out=counts[:, 1, n:n + 1]).then_inc(counted, 1)
                        else:
                            dve.memset(counts[:, 1, 0:1], 0.0).then_inc(counted, 1)
                        wait(dve, counted, k + 2)
                        dve.scalar_tensor_tensor(out=rank_junk[:, 0:P], in0=score_row[:, n * P:(n + 1) * P],
                                                 scalar=own, in1=before[:], op0=ALU.is_equal, op1=ALU.mult,
                                                 accum_out=counts[:, 2, n:n + 1]).then_inc(counted, 1)
                if on["rank"] and t == 5:
                    r = 6 * (b - 1)
                    wait(dve, counted, 3 * TB * b)
                    wait(dve, perm_scattered, 16 * TB * (b - 1))
                    dve.tensor_tensor(rank_f[:], counts[:, 0, :], counts[:, 1, :], ALU.add).then_inc(rank_step, 1)
                    wait(dve, rank_step, r + 1)
                    dve.tensor_tensor(rank_f[:], rank_f[:], counts[:, 2, :], ALU.add).then_inc(rank_step, 1)
                    wait(dve, rank_step, r + 2)
                    dve.tensor_copy(rank_u[:], rank_f[:])
                    dve.tensor_scalar(chosen[:], rank_f[:], float(K), None, ALU.is_lt)
                    dve.tensor_scalar(route_f[:], rank_f[:], slot_base[:], None, ALU.add).then_inc(rank_step, 1)
                    wait(dve, rank_step, r + 3)
                    dve.tensor_tensor(route_f[:], route_f[:], chosen[:], ALU.mult).then_inc(rank_step, 1)
                    wait(dve, rank_step, r + 4)
                    dve.tensor_scalar(route[0][:], route_f[:], float(ZROW), None, ALU.add)
                    wait(dve, gate_exped, b)
                    dve.tensor_scalar(gate_exp[:], gate_exp[:], 1.0, None, ALU.add).then_inc(rank_step, 1)
                    wait(dve, rank_step, r + 5)
                    dve.reciprocal(gate[0][:], gate_exp[:]).then_inc(rank_step, 1)
                    wait(dve, rank_step, r + 6)
                    dve.memset(rank_junk[:, 0:1], 0.0).then_inc(routed, 1)
                if on["ffn"] and t >= 4:
                    n = (b - 2) * SB_ + t - 4
                    wait(dve, proc_made, n + 1)
                    wait(dve, proc_stored[t % 2], 16 * ((b - 2) * (SB_ // 2) + (t - 4) // 2))
                    dve.tensor_tensor(proc_sb[:, t % 2, :], psP[:, 0:D], b2_sb[:], ALU.add).then_inc(proc_ready, 1)
                if on["attn"]:
                    wait(dve, exp_ready, T + 1)
                    ex = expo[:].rearrange("p (h g) -> p h g", h=H)
                    dve.tensor_reduce(row_sum[:], ex, AX.X, ALU.add).then_inc(sum_ready, 1)
                    wait(dve, sum_ready, T + 1)
                    dve.reciprocal(row_inv[:], row_sum[:]).then_inc(inv_ready, 1)
                    wait(dve, inv_ready, T + 1)
                    wait(dve, pv_pool, T - 1)
                    wait(dve, pv_dve, T - 1)
                    dve.tensor_tensor(probs[:, u, :].rearrange("p (h g) -> p h g", h=H), ex,
                                      row_inv[:].unsqueeze(2).broadcast_to([P, H, H]), ALU.mult
                                      ).then_inc(probs_ready, 1)

            program(dve, step)


_WEIGHTS = ["Wq", "bq", "Wdown", "bdown", "Wup", "Wout", "bout", "w_router", "W1", "b1", "W2", "b2"]


def kernel(L0_attn_x, L0_attn_Wq, L0_attn_bq, L0_attn_Wdown, L0_attn_bdown, L0_attn_Wup, L0_attn_bup, L0_attn_Wout,
           L0_attn_bout, L0_ffn_w_router, L0_ffn_W1, L0_ffn_b1, L0_ffn_W2, L0_ffn_b2):
    import numpy as np
    import concourse.bacc as bacc
    from concourse.bass_utils import run_bass_kernel_spmd

    Bn, Sn, Dn = L0_attn_x.shape
    x = np.asarray(L0_attn_x).reshape(Bn * Sn, Dn)
    xT = x.reshape(Bn * Sn // P, P, Dn // P, P).transpose(0, 3, 2, 1).reshape(Bn * Sn, Dn)
    pad = np.zeros((2 * P, Dn), x.dtype)
    arrays = {
        "xT": np.ascontiguousarray(np.concatenate([xT, pad])), "x": np.ascontiguousarray(np.concatenate([x, pad])),
        "Wq": L0_attn_Wq, "bq": np.asarray(L0_attn_bq)[None, :], "Wdown": L0_attn_Wdown,
        "bdown": np.asarray(L0_attn_bdown)[:, None],
        "Wup": np.concatenate([np.asarray(L0_attn_Wup), np.asarray(L0_attn_bup)[None, :]]),
        "Wout": L0_attn_Wout, "bout": np.asarray(L0_attn_bout)[None, :], "w_router": np.asarray(L0_ffn_w_router)[None, :],
        "W1": L0_ffn_W1, "b1": np.asarray(L0_ffn_b1).reshape(-1, P).T, "W2": L0_ffn_W2,
        "b2": np.asarray(L0_ffn_b2)[None, :],
    }
    arrays = {k: np.ascontiguousarray(v) for k, v in arrays.items()}
    nc = bacc.Bacc("TRN2", target_bir_lowering=False, num_devices=1)
    ap = {k: nc.dram_tensor(k, v.shape, mybir.dt.from_np(v.dtype), kind="ExternalInput").ap()
          for k, v in arrays.items()}
    out = nc.dram_tensor("out", (Bn * Sn, Dn), F32, kind="ExternalOutput").ap()
    x1_dram = nc.dram_tensor("x1_dram", (Bn * Sn, Dn), F32, kind="Internal").ap()
    score_dram = nc.dram_tensor("score_dram", (1, Sn), F32, kind="Internal").ap()
    perm_dram = nc.dram_tensor("perm_dram", (Sn, 1), U32, kind="Internal").ap()
    proc_dram = nc.dram_tensor("proc_dram", (Bn * Sn // 2 + 1, Dn), F32, kind="Internal").ap()
    build_layer(nc, ap["xT"], ap["x"], *[ap[k] for k in _WEIGHTS], out, x1_dram, score_dram, perm_dram, proc_dram)
    r = run_bass_kernel_spmd(nc, [arrays], core_ids=[0])
    return r.results[0]["out"].reshape(Bn, Sn, Dn)
```

```python
from contextlib import ExitStack

import concourse.bass as bass
from concourse import mybir

F32 = mybir.dt.float32
BF16 = mybir.dt.bfloat16
U32 = mybir.dt.uint32
ALU = mybir.AluOpType
ACT = mybir.ActivationFunctionType
AX = mybir.AxisListType

P = 128
EPS = 1e-5


def build_layer(nc, xT, x, Wq, Wdown, bdown, Wup, Wout, biases, w_router, W1, b1, W2, out,
                x1_dram, score_dram, chosen_dram, proc_dram):
    N, D = out.shape
    H, DH = 16, D // 16
    L = Wdown.shape[1]
    F = W1.shape[1]
    S = 1024
    B = N // S
    TB = S // P
    K = S // 2
    SB_ = K // P
    KD = D // P
    FT = F // P
    PAIRS = H * H * DH
    ZROW = B * K
    TILES = B * TB
    QH_POOL = 9
    PG_POOL = 9
    SCALE = float(DH) ** -0.5

    with ExitStack() as ctx:
        def sb(name, shape, dt=F32):
            return ctx.enter_context(nc.sbuf_tensor(name, shape, dt))

        def ps(name):
            return ctx.enter_context(nc.psum_tensor(name, [P, 512], F32))

        def sem(name):
            return ctx.enter_context(nc.semaphore(name))

        wq_sb = sb("wq_sb", [P, KD, D])
        wdown_sb = sb("wdown_sb", [P, KD, L])
        wup_sb = sb("wup_sb", [L + 1, 2 * D])
        wout_sb = sb("wout_sb", [P, KD, D])
        w1_sb = sb("w1_sb", [P, KD, F])
        w2_sb = sb("w2_sb", [P, FT, D])
        bdown_sb = sb("bdown_sb", [L, 1])
        b1_sb = sb("b1_sb", [P, FT])
        router_sb = sb("router_sb", [P, D])
        bias_sb = sb("bias_sb", [1, 3 * D])
        bias_rest = sb("bias_rest", [1, 3 * D])
        bias_cut = sb("bias_cut", [1, 3, 3 * D], BF16)
        bias_parts = sb("bias_parts", [3, 3 * D], BF16)
        ones_parts = sb("ones_parts", [3, P], BF16)
        ones_col = sb("ones_col", [P, 1], BF16)
        ident = sb("ident", [P, P])
        after = sb("after", [P, P])
        minus_half = sb("minus_half", [P, 1])
        zero_rows = sb("zero_rows", [P, 4 * D])

        xT_sb = sb("xT_sb", [P, 4, KD, P])
        x_sb = sb("x_sb", [P, 4, D])
        latT_sb = sb("latT_sb", [L + 1, P])
        q_sb = sb("q_sb", [P, 2, D])
        kv_sb = sb("kv_sb", [P, 4, 2 * D])
        qk_prod = sb("qk_prod", [P, 2, PAIRS])
        logits = sb("logits", [P, H * H])
        neg_max = sb("neg_max", [P, H])
        expo = sb("expo", [P, H * H])
        row_sum = sb("row_sum", [P, H])
        row_inv = sb("row_inv", [P, H])
        probs = sb("probs", [P, 2, H * H])
        pv_prod = sb("pv_prod", [P, 2, PAIRS])
        oT_sb = sb("oT_sb", [P, KD, P])
        resid = sb("resid", [P, D])
        stats = sb("stats", [P, 6])
        mean_var = sb("mean_var", [P, 2])
        var_eps = sb("var_eps", [P, 1])
        rstd = sb("rstd", [P, 1])
        x1_sb = sb("x1_sb", [P, 4, D])
        score_junk = sb("score_junk", [P, D])

        score_new = sb("score_new", [P, TB])
        score_old = sb("score_old", [P, TB])
        score_row = sb("score_row", [P, S])
        beats = sb("beats", [P, 2, S], BF16)
        ties = sb("ties", [P, 2, P], BF16)
        rank_f = sb("rank_f", [P, TB])
        rank_u = sb("rank_u", [P, TB], U32)
        chosen = sb("chosen", [P, TB])
        route_f = sb("route_f", [P, TB])
        route = [sb(f"route{i}", [P, TB], U32) for i in range(3)]
        gate_exp = sb("gate_exp", [P, TB])
        gate = [sb(f"gate{i}", [P, TB]) for i in range(3)]
        slot_base = sb("slot_base", [P, 1])
        x1_batch = sb("x1_batch", [P, TB, D])
        chosen_x = sb("chosen_x", [P, SB_, D])
        chosenT = sb("chosenT", [P, KD, K])
        hidT = sb("hidT", [P, FT, K])
        proc_sb = sb("proc_sb", [P, 2, D])
        x1_back = sb("x1_back", [P, 2, D])
        upd = sb("upd", [P, 2, D])
        upd_gated = sb("upd_gated", [P, D])
        z_sb = sb("z_sb", [P, 2, D])
        z_stats = sb("z_stats", [P, 6])
        z_mean_var = sb("z_mean_var", [P, 2, 2])
        z_var_eps = sb("z_var_eps", [P, 2])
        z_rstd = sb("z_rstd", [P, 2])
        out_sb = sb("out_sb", [P, 2, D])

        psQ, psKV, psO, psW, psF0, psF1, psP, psR = [ps(n) for n in
            ("psQ", "psKV", "psO", "psW", "psF0", "psF1", "psP", "psR")]
        psF = [psF0, psF1]

        proj_loaded, rest_loaded, parts_loaded = sem("proj_loaded"), sem("rest_loaded"), sem("parts_loaded")
        xT_loaded = [sem(f"xT_loaded{i}") for i in range(4)]
        x_loaded = [sem(f"x_loaded{i}") for i in range(4)]
        x1_stored = [sem(f"x1_stored{i}") for i in range(4)]
        score_stored, row_loaded, batch_loaded = sem("score_stored"), sem("row_loaded"), sem("batch_loaded")
        chosen_scattered, chosen_loaded = sem("chosen_scattered"), sem("chosen_loaded")
        zero_stored = sem("zero_stored")
        proc_stored = [sem(f"proc_stored{i}") for i in range(2)]
        x1_back_loaded = [sem(f"x1_back_loaded{i}") for i in range(2)]
        out_stored = [sem(f"out_stored{i}") for i in range(2)]
        upd_gathered = [sem(f"upd_gathered{i}") for i in range(2)]
        passed = {"DVE": sem("dve_passed"), "Pool": sem("pool_passed"), "SP": sem("sp_passed")}
        pool_cleared, consts_ready, dve_consts = sem("pool_cleared"), sem("consts_ready"), sem("dve_consts")
        bias_step = sem("bias_step")
        lat_made, lat_copied = sem("lat_made"), sem("lat_copied")
        q_made, q_copied, kv_made, kv_copied = sem("q_made"), sem("q_copied"), sem("kv_made"), sem("kv_copied")
        qk_pool, qk_dve, logits_ready = sem("qk_pool"), sem("qk_dve"), sem("logits_ready")
        max_ready, exp_ready = sem("max_ready"), sem("exp_ready")
        inv_ready, probs_ready = sem("inv_ready"), sem("probs_ready")
        pv_pool, pv_dve, oT_made, oT_copied = sem("pv_pool"), sem("pv_dve"), sem("oT_made"), sem("oT_copied")
        attn_made, resid_ready, stats_ready = sem("attn_made"), sem("resid_ready"), sem("stats_ready")
        mv_ready, var_ready, rstd_ready = sem("mv_ready"), sem("var_ready"), sem("rstd_ready")
        x1_ready, score_ready = sem("x1_ready"), sem("score_ready")
        gated_ready, z_ready, zstats_ready = sem("gated_ready"), sem("z_ready"), sem("zstats_ready")
        zmv_ready, zvar_ready, zrstd_ready = sem("zmv_ready"), sem("zvar_ready"), sem("zrstd_ready")
        out_ready = sem("out_ready")
        score_kept, compared, ranked = sem("score_kept"), sem("compared"), sem("ranked")
        rank_added = sem("rank_added")
        rank_step, routed, shifted_route, gate_exped = sem("rank_step"), sem("routed"), sem("shifted_route"), sem("gate_exped")
        chosenT_made, chosenT_copied = sem("chosenT_made"), sem("chosenT_copied")
        hid_made, hid_ready, proc_made, proc_ready = sem("hid_made"), sem("hid_ready"), sem("proc_made"), sem("proc_ready")

        def wait(eng, s, value):
            if not (isinstance(value, int) and value <= 0):
                eng.wait_ge(s, value)

        def wait_alone(eng, s, value):
            wait(eng, s, value)
            if not isinstance(value, int):
                eng.sem_inc(passed[eng.engine.name], 1)

        N_PROJ, N_REST = 5, 6
        N_ZERO = 1 + 2 * B * K // S
        QK, SM, PV, OUT, NORM = 1, 2, 3, 4, 5
        LAST = 3 * TB
        FIRST = 4

        def has(T, lag):
            return not isinstance(T, int) or 0 <= T - lag < TILES

        def batch(b, lag):
            return not isinstance(b, int) or 0 <= b - lag < B

        def program(eng, step):
            for b in range(FIRST):
                for t in range(TB):
                    step(b, t)
            with eng.Fori(FIRST, B) as b:
                for t in range(TB):
                    step(b, t)
            for b in range(B, B + 4):
                for t in range(TB):
                    step(b, t)

        def hidden_tiles(t):
            return (2 * t - 2, 2 * t - 1) if 1 <= t <= 4 else ()

        def slot_tiles(t):
            return {5: (0,), 6: (1,), 7: (2, 3)}.get(t, ())

        block = ctx.enter_context(nc.Block())

        @block.sync
        def _(sp):
            def load_xT(T, t):
                wait_alone(sp, lat_made, T - 3)
                wait_alone(sp, q_made, T - 3)
                sp.dma_start(xT_sb[:, t % 4, :, :], xT[bass.ds(T * P, P), :].rearrange("k (a n) -> k a n", a=KD)
                             ).then_inc(xT_loaded[t % 4], 16)

            sp.dma_start(wdown_sb[:], Wdown.rearrange("(a k) n -> k a n", a=KD)).then_inc(proj_loaded, 16)
            load_xT(0, 0)
            sp.dma_start(bdown_sb[:], bdown).then_inc(proj_loaded, 16)
            sp.dma_start(wq_sb[:], Wq.rearrange("(a k) n -> k a n", a=KD)).then_inc(proj_loaded, 16)
            sp.dma_start(bias_sb[:], biases).then_inc(proj_loaded, 16)
            sp.dma_start(wup_sb[:], Wup).then_inc(proj_loaded, 16)
            load_xT(1, 1)
            sp.wait_ge(bias_step, 5)
            for c in range(3):
                sp.dma_start(bias_parts[c:c + 1, :], bias_cut[:, c, :]).then_inc(parts_loaded, 16)
            sp.dma_start(wout_sb[:], Wout.rearrange("(a k) n -> k a n", a=KD)).then_inc(rest_loaded, 16)
            sp.dma_start(router_sb[:], w_router.broadcast_to([P, D])).then_inc(rest_loaded, 16)
            sp.dma_start(b1_sb[:], b1).then_inc(rest_loaded, 16)
            half = F // 2
            for c in range(2):
                sp.dma_start(w1_sb[:, :, c * half:(c + 1) * half],
                             W1[:, c * half:(c + 1) * half].rearrange("(a k) n -> k a n", a=KD)
                             ).then_inc(rest_loaded, 16)
            sp.dma_start(w2_sb[:], W2.rearrange("(a k) n -> k a n", a=FT)).then_inc(rest_loaded, 16)

            def step(b, t):
                T = b * TB + t
                if has(T, 0):
                    load_xT(T + 2, t + 2)
                if has(T, OUT - 1):
                    i = T - OUT + 1
                    c = (t - OUT + 1) % 4
                    wait_alone(sp, resid_ready, i - 3)
                    sp.dma_start(x_sb[:, c, :], x[bass.ds(i * P, P), :]).then_inc(x_loaded[c], 16)
                if has(T, LAST):
                    f = T - LAST
                    wait_alone(sp, z_ready, f - 1)
                    sp.dma_start(x1_back[:, t % 2, :], x1_dram[bass.ds(f * P, P), :]
                                 ).then_inc(x1_back_loaded[t % 2], 16)
                if has(T, LAST + 2):
                    f = T - LAST - 2
                    wait_alone(sp, out_ready, f + 1)
                    sp.dma_start(out[bass.ds(f * P, P), :], out_sb[:, t % 2, :]).then_inc(out_stored[t % 2], 16)
                if has(T, NORM):
                    i = T - NORM
                    c = (t - NORM) % 4
                    wait_alone(sp, x1_ready, i + 1)
                    sp.dma_start(x1_dram[bass.ds(i * P, P), :], x1_sb[:, c, :]).then_inc(x1_stored[c], 16)
                if batch(b, 1) and t == 4:
                    wait_alone(sp, score_kept, b)
                    sp.dma_start(score_dram.rearrange("a (t p) -> (a p) t", p=P), score_old[:],
                                 allow_slow_non_contiguous=True).then_inc(score_stored, 16)
                    wait_alone(sp, score_stored, 16 * b)
                    wait_alone(sp, compared, TB * (b - 1))
                    sp.dma_start(score_row[:], score_dram.broadcast_to([P, S])).then_inc(row_loaded, 16)
                if batch(b, 1) and t == 5:
                    for c in range(4):
                        wait_alone(sp, x1_stored[c], 16 * TB // 4 * b)
                    wait_alone(sp, chosen_scattered, 16 * TB * (b - 1))
                    sp.dma_start(x1_batch[:], x1_dram[bass.ds((b - 1) * S, S), :].rearrange("(n p) d -> p n d", p=P)
                                 ).then_inc(batch_loaded, 16)
                if batch(b, 2) and t == 0:
                    wait_alone(sp, chosen_scattered, 16 * TB * (b - 1))
                    wait_alone(sp, chosenT_made, KD * (b - 2))
                    sp.dma_start(chosen_x[:], chosen_dram.rearrange("(s p) d -> p s d", p=P)
                                 ).then_inc(chosen_loaded, 16)
                if batch(b, 2):
                    if t == 5 and isinstance(b, int) and b == 2:
                        sp.wait_ge(zero_stored, 16 * N_ZERO)
                    for s in slot_tiles(t):
                        n = (b - 2) * SB_ + s
                        wait_alone(sp, proc_ready, n + 1)
                        sp.dma_start(proc_dram[bass.ds(n * P, P), :], proc_sb[:, s % 2, :]
                                     ).then_inc(proc_stored[s % 2], 16)
                if isinstance(b, int) and b == 0 and t == 0:
                    sp.wait_ge(dve_consts, 1)
                    sp.dma_start(proc_dram[ZROW:ZROW + 1, :], zero_rows[0:1, 0:D]).then_inc(zero_stored, 16)
                    rows = S // 2
                    for n in range(B * K // rows):
                        sp.dma_start(proc_dram[n * rows:(n + 1) * rows, :].rearrange("(p a) d -> p (a d)", p=P),
                                     zero_rows[:]).then_inc(zero_stored, 16)

            program(sp, step)
            for c in range(2):
                sp.wait_ge(out_stored[c], 16 * TILES // 2)
                sp.wait_ge(proc_stored[c], 16 * B * SB_ // 2)
                sp.wait_ge(xT_loaded[c], 16 * (TILES // 4 + 1))
            for c in range(4):
                sp.wait_ge(x1_stored[c], 16 * TILES // 4)

        @block.tensor
        def _(pe):
            def bias_rows(acc, n):
                pe.matmul(acc[:, 0:D], ones_parts[:], bias_parts[:, n * D:(n + 1) * D], start=True, stop=False)

            def step(b, t):
                T = b * TB + t
                if has(T, 0):
                    c = t % 4
                    wait(pe, xT_loaded[c], 16 * (2 * b + t // 4 + 1))
                    wait(pe, kv_copied, T)
                    for a in range(KD):
                        mm = pe.matmul(psKV[0:L, 0:P], wdown_sb[:, a, :], xT_sb[:, c, a, :],
                                       start=(a == 0), stop=(a == KD - 1))
                    mm.then_inc(lat_made, 1)
                    if isinstance(T, int) and T == 0:
                        pe.wait_ge(parts_loaded, 48)
                    wait(pe, q_copied, T)
                    bias_rows(psQ, 0)
                    for a in range(KD):
                        mm = pe.matmul(psQ[:, 0:D], xT_sb[:, c, a, :], wq_sb[:, a, :],
                                       start=False, stop=(a == KD - 1))
                    mm.then_inc(q_made, 1)
                if isinstance(T, int) and T == OUT:
                    pe.wait_ge(rest_loaded, 16 * N_REST)
                if has(T, OUT):
                    i = T - OUT
                    wait(pe, oT_copied, i + 1)
                    wait(pe, resid_ready, i)
                    bias_rows(psW, 1)
                    for a in range(KD):
                        mm = pe.matmul(psW[:, 0:D], oT_sb[:, a, :], wout_sb[:, a, :],
                                       start=False, stop=(a == KD - 1))
                    mm.then_inc(attn_made, 1)
                if has(T, 0):
                    wait(pe, lat_copied, T + 1)
                    pe.matmul(psKV[:], latT_sb[:], wup_sb[:], start=True, stop=True).then_inc(kv_made, 1)
                if batch(b, 2) and t == 1:
                    wait(pe, chosen_loaded, 16 * (b - 1))
                    wait(pe, hid_ready, (b - 2) * FT)
                    for a in range(KD):
                        for s in range(SB_):
                            mm = pe.transpose(psF[a][:, s * P:(s + 1) * P], chosen_x[:, s, a * P:(a + 1) * P], ident[:])
                        mm.then_inc(chosenT_made, 1)
                if batch(b, 2):
                    for f in hidden_tiles(t):
                        n = (b - 2) * FT + f
                        wait(pe, hid_ready, n - 1)
                        if f < 2:
                            wait(pe, chosenT_copied, KD * (b - 1))
                        for a in range(KD):
                            mm = pe.matmul(psF[f % 2][:], w1_sb[:, a, f * P:(f + 1) * P], chosenT[:, a, :],
                                           start=(a == 0), stop=(a == KD - 1))
                        mm.then_inc(hid_made, 1)
                    for s in slot_tiles(t):
                        n = (b - 2) * SB_ + s
                        wait(pe, hid_ready, (b - 1) * FT)
                        wait(pe, proc_ready, n)
                        bias_rows(psP, 2)
                        for f in range(FT):
                            mm = pe.matmul(psP[:, 0:D], hidT[:, f, s * P:(s + 1) * P], w2_sb[:, f, :],
                                           start=False, stop=(f == FT - 1))
                        mm.then_inc(proc_made, 1)
                if has(T, PV):
                    i = T - PV
                    u = (t - PV) % 2
                    wait(pe, oT_copied, i)
                    for a in range(KD):
                        for n, g in enumerate([*range(PG_POOL, H), *range(PG_POOL)]):
                            if a == 0 and n == 0:
                                wait(pe, pv_dve, i + 1)
                            if a == 0 and g == 0:
                                wait(pe, pv_pool, i + 1)
                            mm = pe.matmul(psO[:, a * P:(a + 1) * P],
                                           pv_prod[:, u, g * D + a * P:g * D + (a + 1) * P], ident[:],
                                           start=(n == 0), stop=(n == H - 1), is_transpose=True)
                    mm.then_inc(oT_made, 1)
                if batch(b, 1) and t in (4, 5):
                    for j in range(4 * t - 16, 4 * t - 12):
                        wait(pe, compared, TB * (b - 1) + j + 1)
                        if j == 0:
                            wait(pe, ranked, b - 1)
                        for n in range(TB):
                            mm = pe.matmul(psR[:, n:n + 1], beats[:, j % 2, n * P:(n + 1) * P], ones_col[:],
                                           start=(j == 0 and n == 0), stop=False, skip_group_check=True)
                        mm = pe.matmul(psR[:, j:j + 1], ties[:, j % 2, :], ones_col[:],
                                       start=False, stop=(j == TB - 1), skip_group_check=True)
                        mm.then_inc(rank_added, 1)

            pe.wait_ge(proj_loaded, 16 * N_PROJ)
            pe.wait_ge(consts_ready, 1)
            pe.wait_ge(dve_consts, 1)
            program(pe, step)

        @block.scalar
        def _(act):
            def step(b, t):
                T = b * TB + t
                if has(T, 0):
                    wait(act, lat_made, T + 1)
                    wait(act, kv_made, T)
                    nc.scalar.activation(latT_sb[0:L, :], psKV[0:L, 0:P], ACT.Identity, bias=bdown_sb[:]
                                         ).then_inc(lat_copied, 1)
                    wait(act, q_made, T + 1)
                    wait(act, qk_dve, T - 1)
                    wait(act, qk_pool, T - 1)
                    nc.scalar.activation(q_sb[:, t % 2, :], psQ[:, 0:D], ACT.Copy, scale=SCALE).then_inc(q_copied, 1)
                    wait(act, kv_made, T + 1)
                    wait(act, pv_dve, T - 3)
                    wait(act, pv_pool, T - 3)
                    nc.scalar.activation(kv_sb[:, t % 4, :], psKV[:], ACT.Copy).then_inc(kv_copied, 1)
                if batch(b, 1) and t == 5:
                    wait(act, score_kept, b)
                    wait(act, routed, b - 1)
                    nc.scalar.activation(gate_exp[:], score_old[:], ACT.Exp, scale=-1.0).then_inc(gate_exped, 1)
                if has(T, SM):
                    i = T - SM
                    wait(act, max_ready, i + 1)
                    wait(act, probs_ready, i)
                    for h in range(H):
                        e = nc.scalar.activation(expo[:, h * H:(h + 1) * H], logits[:, h * H:(h + 1) * H], ACT.Exp,
                                                 bias=neg_max[:, h:h + 1], accum_out=row_sum[:, h:h + 1])
                    e.then_inc(exp_ready, 1)
                if has(T, LAST):
                    f = T - LAST
                    wait(act, upd_gathered[t % 2], 16 * ((b - 3) * (TB // 2) + t // 2 + 1))
                    wait(act, shifted_route, 2 * (b - 1))
                    wait(act, z_ready, f)
                    nc.scalar.activation(upd_gated[:], upd[:, t % 2, :], ACT.Copy, scale=gate[2][:, t:t + 1]
                                         ).then_inc(gated_ready, 1)
                if batch(b, 2):
                    if t == 1:
                        for a in range(KD):
                            wait(act, chosenT_made, KD * (b - 2) + a + 1)
                            wait(act, hid_made, (b - 2) * FT)
                            nc.scalar.activation(chosenT[:, a, :], psF[a][:], ACT.Copy).then_inc(chosenT_copied, 1)
                    for f in hidden_tiles(t):
                        wait(act, hid_made, (b - 2) * FT + f + 1)
                        wait(act, proc_made, (b - 2) * SB_)
                        nc.scalar.activation(hidT[:, f, :], psF[f % 2][:], ACT.Gelu_apprx_tanh,
                                             bias=b1_sb[:, f:f + 1]).then_inc(hid_ready, 1)
                    for s in slot_tiles(t):
                        wait(act, proc_made, (b - 2) * SB_ + s + 1)
                        wait(act, proc_stored[s % 2], 16 * ((b - 2) * (SB_ // 2) + s // 2))
                        nc.scalar.activation(proc_sb[:, s % 2, :], psP[:, 0:D], ACT.Copy).then_inc(proc_ready, 1)
                if has(T, PV):
                    i = T - PV
                    wait(act, oT_made, i + 1)
                    wait(act, attn_made, i)
                    nc.scalar.activation(oT_sb[:], psO[:, 0:D].rearrange("p (a n) -> p a n", a=KD), ACT.Copy
                                         ).then_inc(oT_copied, 1)

            act.wait_ge(proj_loaded, 16 * N_PROJ)
            program(act, step)

        def heads(ap, h0, h1):
            return ap.rearrange("p (h d) -> p h d", h=H)[:, h0:h1, :].unsqueeze(2).broadcast_to([P, h1 - h0, H, DH])

        def qk_products(eng, t, h0, h1):
            u = t % 2
            keys = kv_sb[:, t % 4, :].rearrange("p (g e) -> p g e", g=H)[:, :, 0:DH]
            return eng.tensor_tensor(
                qk_prod[:, u, h0 * H * DH:h1 * H * DH].rearrange("p (h g d) -> p h g d", h=h1 - h0, g=H),
                heads(q_sb[:, u, :], h0, h1), keys.unsqueeze(1).broadcast_to([P, h1 - h0, H, DH]), ALU.mult)

        def pv_products(eng, t, g0, g1):
            u = t % 2
            weight = probs[:, u, :].rearrange("p (h g) -> p g h", h=H)[:, g0:g1, :]
            values = kv_sb[:, t % 4, :].rearrange("p (g e) -> p g e", g=H)[:, g0:g1, DH:2 * DH]
            return eng.tensor_tensor(
                pv_prod[:, u, g0 * H * DH:g1 * H * DH].rearrange("p (g h d) -> p g h d", g=g1 - g0, h=H),
                weight.unsqueeze(3).broadcast_to([P, g1 - g0, H, DH]),
                values.unsqueeze(2).broadcast_to([P, g1 - g0, H, DH]), ALU.mult)

        @block.gpsimd
        def _(pool):
            pool.memset(ident[:], 0.0).then_inc(pool_cleared, 1)
            pool.memset(after[:], 1.0).then_inc(pool_cleared, 1)
            pool.wait_ge(pool_cleared, 2)
            pool.affine_select(out=ident[:], in_=ident[:], compare_op=ALU.not_equal, fill=1.0, base=0,
                               pattern=[[-1, P]], channel_multiplier=1).then_inc(pool_cleared, 1)
            pool.affine_select(out=after[:], in_=after[:], compare_op=ALU.is_gt, fill=0.0, base=0,
                               pattern=[[1, P]], channel_multiplier=-1).then_inc(pool_cleared, 1)
            pool.wait_ge(pool_cleared, 4)
            pool.memset(minus_half[:], -0.5).then_inc(consts_ready, 1)
            pool.wait_ge(dve_consts, 1)
            pool.wait_ge(consts_ready, 1)

            def step(b, t):
                T = b * TB + t
                if has(T, PV):
                    i = T - PV
                    wait(pool, probs_ready, i + 1)
                    wait(pool, oT_made, i - 1)
                    pv_products(pool, t - PV, 0, PG_POOL).then_inc(pv_pool, 1)
                if has(T, LAST):
                    f = T - LAST
                    if t == 0:
                        for c in range(2):
                            wait(pool, proc_stored[c], (b - 2) * (16 * SB_ // 2))
                        wait(pool, zero_stored, 16 * N_ZERO)
                        wait(pool, shifted_route, 2 * (b - 1))
                    wait_alone(pool, gated_ready, f - 1)
                    pool.indirect_dma_start(upd[:, t % 2, :], None, proc_dram,
                                            bass.IndirectOffsetOnAxis(route[2][:, t:t + 1], 0)
                                            ).then_inc(upd_gathered[t % 2], 16)
                if has(T, QK):
                    i = T - QK
                    wait(pool, q_copied, i + 1)
                    wait(pool, kv_copied, i + 1)
                    wait(pool, logits_ready, 2 * (i - 1))
                    qk_products(pool, t - QK, 0, QH_POOL).then_inc(qk_pool, 1)
                if has(T, OUT):
                    i = T - OUT
                    wait(pool, var_ready, i + 1)
                    wait(pool, x1_ready, i)
                    pool.tensor_tensor(rstd[:], var_eps[:], minus_half[:], ALU.pow).then_inc(rstd_ready, 1)
                if has(T, LAST + 1):
                    f = T - LAST - 1
                    c = (t - 1) % 2
                    wait(pool, zvar_ready, f + 1)
                    wait(pool, out_ready, f - 1)
                    pool.tensor_tensor(z_rstd[:, c:c + 1], z_var_eps[:, c:c + 1], minus_half[:], ALU.pow
                                       ).then_inc(zrstd_ready, 1)
                if batch(b, 1) and t in (6, 7):
                    if t == 6:
                        wait(pool, routed, b)
                        wait(pool, batch_loaded, 16 * b)
                        wait_alone(pool, chosen_loaded, 16 * (b - 1))
                    for n in range(4 * t - 24, 4 * t - 20):
                        pool.indirect_dma_start(chosen_dram, bass.IndirectOffsetOnAxis(rank_u[:, n:n + 1], 0),
                                                x1_batch[:, n, :], None, bounds_check=K - 1, oob_is_err=False
                                                ).then_inc(chosen_scattered, 16)

            program(pool, step)

        @block.vector
        def _(dve):
            dve.memset(latT_sb[L:L + 1, :], 1.0)
            dve.memset(ones_parts[:], 1.0)
            dve.memset(ones_col[:], 1.0)
            dve.memset(slot_base[:], float(-ZROW))
            dve.memset(zero_rows[:], 0.0).then_inc(dve_consts, 1)
            dve.wait_ge(proj_loaded, 16 * N_PROJ)
            dve.tensor_copy(bias_cut[:, 0, :], bias_sb[:]).then_inc(bias_step, 1)
            dve.wait_ge(bias_step, 1)
            dve.tensor_tensor(bias_rest[:], bias_sb[:], bias_cut[:, 0, :], ALU.subtract).then_inc(bias_step, 1)
            dve.wait_ge(bias_step, 2)
            dve.tensor_copy(bias_cut[:, 1, :], bias_rest[:]).then_inc(bias_step, 1)
            dve.wait_ge(bias_step, 3)
            dve.tensor_tensor(bias_rest[:], bias_rest[:], bias_cut[:, 1, :], ALU.subtract).then_inc(bias_step, 1)
            dve.wait_ge(bias_step, 4)
            dve.tensor_copy(bias_cut[:, 2, :], bias_rest[:]).then_inc(bias_step, 1)
            dve.wait_ge(consts_ready, 1)

            def reduce_logits(u, h0, h1):
                return dve.tensor_reduce(
                    logits[:, h0 * H:h1 * H],
                    qk_prod[:, u, h0 * H * DH:h1 * H * DH].rearrange("p (n d) -> p n d", d=DH), AX.X, ALU.add)

            def step(b, t):
                T = b * TB + t
                if t == 0 and (batch(b, 2) or batch(b, 3)):
                    wait(dve, gated_ready, (b - 3) * TB)
                    for c in range(2):
                        wait(dve, upd_gathered[c], (b - 3) * (16 * TB // 2))
                    if batch(b, 3):
                        dve.tensor_copy(route[2][:], route[1][:])
                        dve.tensor_copy(gate[2][:], gate[1][:]).then_inc(shifted_route, 1)
                    else:
                        dve.memset(route[2][:], 0)
                        dve.memset(gate[2][:], 0.0).then_inc(shifted_route, 1)
                    if batch(b, 2):
                        dve.wait_ge(shifted_route, 2 * b - 3)
                        dve.tensor_copy(route[1][:], route[0][:])
                        dve.tensor_copy(gate[1][:], gate[0][:]).then_inc(shifted_route, 1)
                    else:
                        dve.wait_ge(shifted_route, 2 * b - 3)
                        dve.memset(gate[1][:], 0.0).then_inc(shifted_route, 1)
                if t == 0 and batch(b, 2) and batch(b, 1):
                    dve.tensor_scalar(slot_base[:], slot_base[:], float(K), None, ALU.add)
                if has(T, NORM):
                    i = T - NORM
                    c = (t - NORM) % 4
                    if isinstance(T, int) and T == NORM:
                        dve.wait_ge(rest_loaded, 16 * N_REST)
                    wait(dve, rstd_ready, i + 1)
                    wait(dve, x1_stored[c], 16 * (2 * b + (t - NORM) // 4))
                    dve.tensor_scalar(x1_sb[:, c, :], resid[:], mean_var[:, 0:1], rstd[:, 0:1],
                                      ALU.subtract, ALU.mult).then_inc(x1_ready, 1)
                if has(T, LAST + 2):
                    f = T - LAST - 2
                    wait(dve, zrstd_ready, f + 1)
                    wait(dve, out_stored[t % 2], 16 * ((b - 3) * (TB // 2) + (t - 2) // 2))
                    dve.tensor_scalar(out_sb[:, t % 2, :], z_sb[:, t % 2, :], z_mean_var[:, t % 2, 0:1],
                                      z_rstd[:, t % 2:t % 2 + 1], ALU.subtract, ALU.mult).then_inc(out_ready, 1)
                if has(T, NORM):
                    wait(dve, x1_ready, i + 1)
                    wait(dve, score_ready, i)
                    if t == NORM:
                        wait(dve, score_kept, b)
                    n = (t - NORM) % TB
                    dve.tensor_tensor_reduce(out=score_junk[:], in0=x1_sb[:, c, :], in1=router_sb[:], scale=1.0,
                                             scalar=0.0, op0=ALU.mult, op1=ALU.add,
                                             accum_out=score_new[:, n:n + 1]).then_inc(score_ready, 1)
                if batch(b, 1) and t == 4:
                    wait(dve, score_ready, TB * b)
                    wait(dve, score_stored, 16 * (b - 1))
                    wait(dve, gate_exped, b - 1)
                    wait(dve, compared, TB * (b - 1))
                    dve.tensor_copy(score_old[:], score_new[:]).then_inc(score_kept, 1)
                if has(T, SM):
                    i = T - SM
                    wait(dve, exp_ready, i)
                    wait(dve, qk_dve, i + 1)
                    reduce_logits((t - SM) % 2, QH_POOL, H).then_inc(logits_ready, 1)
                    wait(dve, qk_pool, i + 1)
                    reduce_logits((t - SM) % 2, 0, QH_POOL).then_inc(logits_ready, 1)
                    wait(dve, logits_ready, 2 * (i + 1))
                    dve.tensor_reduce(neg_max[:], logits[:].rearrange("p (h g) -> p h g", h=H), AX.X, ALU.max,
                                      negate=True).then_inc(max_ready, 1)
                if has(T, OUT):
                    i = T - OUT
                    c = (t - OUT) % 4
                    wait(dve, attn_made, i + 1)
                    wait(dve, x_loaded[c], 16 * (2 * b + (t - OUT) // 4 + 1))
                    wait(dve, x1_ready, i)
                    dve.tensor_tensor(resid[:], psW[:, 0:D], x_sb[:, c, :], ALU.add).then_inc(resid_ready, 1)
                if has(T, PV):
                    i = T - PV
                    wait(dve, probs_ready, i + 1)
                    wait(dve, oT_made, i - 1)
                    pv_products(dve, t - PV, PG_POOL, H).then_inc(pv_dve, 1)
                if has(T, OUT):
                    i = T - OUT
                    wait(dve, resid_ready, i + 1)
                    dve.bn_stats(stats[:], resid[:]).then_inc(stats_ready, 1)
                if has(T, QK):
                    i = T - QK
                    wait(dve, q_copied, i + 1)
                    wait(dve, kv_copied, i + 1)
                    wait(dve, logits_ready, 2 * (i - 1))
                    qk_products(dve, t - QK, QH_POOL, H).then_inc(qk_dve, 1)
                if has(T, OUT):
                    i = T - OUT
                    wait_alone(dve, stats_ready, i + 1)
                    dve.bn_aggr(mean_var[:], stats[:]).then_inc(mv_ready, 1)
                if has(T, LAST):
                    f = T - LAST
                    u = t % 2
                    wait(dve, gated_ready, f + 1)
                    wait(dve, x1_back_loaded[u], 16 * ((b - 3) * (TB // 2) + t // 2 + 1))
                    wait(dve, out_ready, f - 1)
                    dve.scalar_tensor_tensor(out=z_sb[:, u, :], in0=x1_back[:, u, :], scalar=2.0, in1=upd_gated[:],
                                             op0=ALU.mult, op1=ALU.add).then_inc(z_ready, 1)
                if has(T, OUT):
                    wait(dve, mv_ready, T - OUT + 1)
                    dve.tensor_scalar(var_eps[:], mean_var[:, 1:2], EPS, None, ALU.add).then_inc(var_ready, 1)
                if has(T, LAST):
                    wait(dve, z_ready, f + 1)
                    wait(dve, zmv_ready, f)
                    dve.bn_stats(z_stats[:], z_sb[:, u, :]).then_inc(zstats_ready, 1)
                    wait_alone(dve, zstats_ready, f + 1)
                    dve.bn_aggr(z_mean_var[:, u, :], z_stats[:]).then_inc(zmv_ready, 1)
                    wait(dve, zmv_ready, f + 1)
                    wait(dve, zrstd_ready, f - 1)
                    dve.tensor_scalar(z_var_eps[:, u:u + 1], z_mean_var[:, u, 1:2], EPS, None, ALU.add
                                      ).then_inc(zvar_ready, 1)
                if batch(b, 1) and t in (4, 5):
                    if t == 4:
                        wait(dve, row_loaded, 16 * b)
                    for j in range(4 * t - 16, 4 * t - 12):
                        own = score_old[:, j:j + 1]
                        wait(dve, rank_added, TB * (b - 1) + j - 1)
                        dve.tensor_scalar(beats[:, j % 2, 0:(j + 1) * P], score_row[:, 0:(j + 1) * P], own, None,
                                          ALU.is_lt)
                        if j < TB - 1:
                            dve.tensor_scalar(beats[:, j % 2, (j + 1) * P:S], score_row[:, (j + 1) * P:S], own, None,
                                              ALU.is_le)
                        dve.scalar_tensor_tensor(out=ties[:, j % 2, :], in0=score_row[:, j * P:(j + 1) * P], scalar=own,
                                                 in1=after[:], op0=ALU.is_equal, op1=ALU.mult).then_inc(compared, 1)
                if has(T, SM):
                    i = T - SM
                    wait(dve, exp_ready, i + 1)
                    dve.reciprocal(row_inv[:], row_sum[:]).then_inc(inv_ready, 1)
                    wait(dve, inv_ready, i + 1)
                    wait(dve, pv_pool, i - 1)
                    wait(dve, pv_dve, i - 1)
                    dve.tensor_tensor(probs[:, (t - SM) % 2, :].rearrange("p (h g) -> p h g", h=H),
                                      expo[:].rearrange("p (h g) -> p h g", h=H),
                                      row_inv[:].unsqueeze(2).broadcast_to([P, H, H]), ALU.mult
                                      ).then_inc(probs_ready, 1)
                if batch(b, 1) and t == 5:
                    r = 5 * (b - 1)
                    wait(dve, rank_added, TB * b)
                    wait(dve, chosen_scattered, 16 * TB * (b - 1))
                    dve.tensor_copy(rank_f[:], psR[:, 0:TB]).then_inc(ranked, 1)
                    wait(dve, ranked, b)
                    dve.tensor_copy(rank_u[:], rank_f[:])
                    dve.tensor_scalar(chosen[:], rank_f[:], float(K), None, ALU.is_lt)
                    dve.tensor_scalar(route_f[:], rank_f[:], slot_base[:], None, ALU.add).then_inc(rank_step, 1)
                    wait(dve, rank_step, r + 1)
                    dve.tensor_tensor(route_f[:], route_f[:], chosen[:], ALU.mult).then_inc(rank_step, 1)
                    wait(dve, gate_exped, b)
                    dve.tensor_scalar(gate_exp[:], gate_exp[:], 1.0, None, ALU.add).then_inc(rank_step, 1)
                    wait(dve, rank_step, r + 2)
                    dve.tensor_scalar(route[0][:], route_f[:], float(ZROW), None, ALU.add).then_inc(rank_step, 1)
                    wait(dve, rank_step, r + 3)
                    dve.reciprocal(gate[0][:], gate_exp[:]).then_inc(rank_step, 1)
                    wait(dve, rank_step, r + 5)
                    dve.tensor_copy(chosen[:], rank_f[:]).then_inc(routed, 1)

            program(dve, step)


_WEIGHTS = ["Wq", "Wdown", "bdown", "Wup", "Wout", "biases", "w_router", "W1", "b1", "W2"]


def kernel(L0_attn_x, L0_attn_Wq, L0_attn_bq, L0_attn_Wdown, L0_attn_bdown, L0_attn_Wup, L0_attn_bup, L0_attn_Wout,
           L0_attn_bout, L0_ffn_w_router, L0_ffn_W1, L0_ffn_b1, L0_ffn_W2, L0_ffn_b2):
    import numpy as np
    import concourse.bacc as bacc
    from concourse.bass_utils import run_bass_kernel_spmd

    Bn, Sn, Dn = L0_attn_x.shape
    x = np.asarray(L0_attn_x).reshape(Bn * Sn, Dn)
    xT = x.reshape(Bn * Sn // P, P, Dn // P, P).transpose(0, 3, 2, 1).reshape(Bn * Sn, Dn)
    pad = np.zeros((2 * P, Dn), x.dtype)
    arrays = {
        "xT": np.ascontiguousarray(np.concatenate([xT, pad])), "x": np.ascontiguousarray(np.concatenate([x, pad])),
        "Wq": L0_attn_Wq, "Wdown": L0_attn_Wdown,
        "biases": np.concatenate([np.asarray(v) for v in (L0_attn_bq, L0_attn_bout, L0_ffn_b2)])[None, :],
        "bdown": np.asarray(L0_attn_bdown)[:, None],
        "Wup": np.concatenate([np.asarray(L0_attn_Wup), np.asarray(L0_attn_bup)[None, :]]),
        "Wout": L0_attn_Wout, "w_router": np.asarray(L0_ffn_w_router)[None, :],
        "W1": L0_ffn_W1, "b1": np.asarray(L0_ffn_b1).reshape(-1, P).T, "W2": L0_ffn_W2,
    }
    arrays = {k: np.ascontiguousarray(v) for k, v in arrays.items()}
    nc = bacc.Bacc("TRN2", target_bir_lowering=False, num_devices=1)
    ap = {k: nc.dram_tensor(k, v.shape, mybir.dt.from_np(v.dtype), kind="ExternalInput").ap()
          for k, v in arrays.items()}
    out = nc.dram_tensor("out", (Bn * Sn, Dn), F32, kind="ExternalOutput").ap()
    x1_dram = nc.dram_tensor("x1_dram", (Bn * Sn, Dn), F32, kind="Internal").ap()
    score_dram = nc.dram_tensor("score_dram", (1, Sn), F32, kind="Internal").ap()
    chosen_dram = nc.dram_tensor("chosen_dram", (Sn // 2, Dn), F32, kind="Internal").ap()
    proc_dram = nc.dram_tensor("proc_dram", (Bn * Sn // 2 + 1, Dn), F32, kind="Internal").ap()
    build_layer(nc, ap["xT"], ap["x"], *[ap[k] for k in _WEIGHTS], out, x1_dram, score_dram, chosen_dram, proc_dram)
    r = run_bass_kernel_spmd(nc, [arrays], core_ids=[0])
    return r.results[0]["out"].reshape(Bn, Sn, Dn)
```

```python
from contextlib import ExitStack

import concourse.bass as bass
from concourse import mybir

F32 = mybir.dt.float32
BF16 = mybir.dt.bfloat16
U32 = mybir.dt.uint32
ALU = mybir.AluOpType
ACT = mybir.ActivationFunctionType
AX = mybir.AxisListType

P = 128
EPS = 1e-5


def build_layer(nc, xT, Wq, Wdown, bdown, Wup, Wout, biases, w_router, W1, b1, W2, out,
                x1_dram, score_dram, chosen_dram, proc_dram):
    N, D = out.shape
    H, DH = 16, D // 16
    L = Wdown.shape[1]
    F = W1.shape[1]
    S = 1024
    B = N // S
    TB = S // P
    K = S // 2
    SB_ = K // P
    KD = D // P
    FT = F // P
    PAIRS = H * H * DH
    ZROW = B * K
    TILES = B * TB
    QH_POOL = (11, 10, 9, 6, 6, 9, 9, 11)
    PG_POOL = (11, 10, 6, 6, 9, 10, 11, 11)
    QH_POOL_FIRST = (9, 8, 9, 8, 9, 8, 9, 10)
    PG_POOL_FIRST = (10, 9, 9, 9, 9, 10, 12, 12)
    SCALE = float(DH) ** -0.5

    with ExitStack() as ctx:
        def sb(name, shape, dt=F32):
            return ctx.enter_context(nc.sbuf_tensor(name, shape, dt))

        def ps(name):
            return ctx.enter_context(nc.psum_tensor(name, [P, 512], F32))

        def sem(name):
            return ctx.enter_context(nc.semaphore(name))

        wq_sb = sb("wq_sb", [P, KD, D])
        wdown_sb = sb("wdown_sb", [P, KD, L])
        wup_sb = sb("wup_sb", [L + 1, 2 * D])
        wout_sb = sb("wout_sb", [P, KD, D])
        w1_sb = sb("w1_sb", [P, KD, F])
        w2_sb = sb("w2_sb", [P, FT, D])
        bdown_sb = sb("bdown_sb", [L, 1])
        b1_sb = sb("b1_sb", [P, FT])
        router_sb = sb("router_sb", [P, D])
        bias_cut = sb("bias_cut", [1, 3, 3 * D], BF16)
        bias_parts = sb("bias_parts", [3, 3 * D], BF16)
        ones_parts = sb("ones_parts", [3, P], BF16)
        ones_col = sb("ones_col", [P, 1], BF16)
        ident = sb("ident", [P, P])
        after = sb("after", [P, P])
        minus_half = sb("minus_half", [P, 2])
        zero_rows = sb("zero_rows", [P, 2 * D])

        xT_sb = sb("xT_sb", [P, TB, KD, P])
        latT_sb = sb("latT_sb", [L + 1, P])
        q_sb = sb("q_sb", [P, 2, D])
        kv_sb = sb("kv_sb", [P, 4, 2 * D])
        qk_prod = sb("qk_prod", [P, 2, PAIRS])
        logits = sb("logits", [P, 2, H * H])
        neg_max = sb("neg_max", [P, 2, H])
        expo = sb("expo", [P, H * H])
        row_sum = sb("row_sum", [P, H])
        row_inv = sb("row_inv", [P, H])
        probs = sb("probs", [P, 2, H * H])
        pv_prod = sb("pv_prod", [P, 2, PAIRS])
        oT_sb = sb("oT_sb", [P, KD, P])
        resid = sb("resid", [P, 2, D])
        total = sb("total", [P, 1])
        neg_mean = sb("neg_mean", [P, 2])
        square_junk = sb("square_junk", [P, D])
        square_sums = sb("square_sums", [P, 2])
        vars_eps = sb("vars_eps", [P, 2])
        rstds = sb("rstds", [P, 2])
        x1_sb = sb("x1_sb", [P, 4, D])
        score_junk = sb("score_junk", [P, D])

        score_new = sb("score_new", [P, TB])
        score_old = sb("score_old", [P, TB])
        score_row = sb("score_row", [P, S])
        beats = sb("beats", [P, TB, S], BF16)
        ties = sb("ties", [P, TB, P], BF16)
        rank_f = sb("rank_f", [P, TB])
        rank_u = sb("rank_u", [P, TB], U32)
        chosen = sb("chosen", [P, TB])
        route_f = sb("route_f", [P, TB])
        route = [sb(f"route{i}", [P, TB], U32) for i in range(3)]
        gate_exp = sb("gate_exp", [P, TB])
        gate_sum = sb("gate_sum", [P, TB])
        gate = [sb(f"gate{i}", [P, TB]) for i in range(3)]
        slot_base = sb("slot_base", [P, 1])
        x1_batch = sb("x1_batch", [P, TB, D])
        bias_sb = x1_batch[0:1, 0:3, :].rearrange("p n d -> p (n d)")
        bias_rest = x1_batch[0:1, 3:6, :].rearrange("p n d -> p (n d)")
        chosen_x = sb("chosen_x", [P, SB_, D])
        chosenT = sb("chosenT", [P, KD, K])
        hidT = sb("hidT", [P, FT, K])
        proc_sb = sb("proc_sb", [P, SB_, D])
        x1_back = sb("x1_back", [P, 4, D])
        upd = sb("upd", [P, 4, D])
        upd_gated = sb("upd_gated", [P, 2, D])
        z_sb = sb("z_sb", [P, 4, D])
        z_total = sb("z_total", [P, 1])
        z_neg_mean = sb("z_neg_mean", [P, 4])
        z_square_junk = sb("z_square_junk", [P, D])
        out_sb = sb("out_sb", [P, 2, D])

        psQ, psKV, psO0, psO1, psW, psF0, psF1, psR = [ps(n) for n in
            ("psQ", "psKV", "psO0", "psO1", "psW", "psF0", "psF1", "psR")]
        psO = [psO0, psO1]
        psF = [psF0, psF1]

        proj_loaded, rest_loaded, parts_loaded = sem("proj_loaded"), sem("rest_loaded"), sem("parts_loaded")
        xT_loaded = [sem(f"xT_loaded{i}") for i in range(TB)]
        x1_stored = [sem(f"x1_stored{i}") for i in range(4)]
        score_stored, row_loaded, batch_loaded = sem("score_stored"), sem("row_loaded"), sem("batch_loaded")
        chosen_scattered, chosen_loaded = sem("chosen_scattered"), sem("chosen_loaded")
        zero_stored = sem("zero_stored")
        proc_stored = [sem(f"proc_stored{i}") for i in range(SB_)]
        x1_back_loaded = [sem(f"x1_back_loaded{i}") for i in range(4)]
        out_stored = [sem(f"out_stored{i}") for i in range(2)]
        upd_gathered = [sem(f"upd_gathered{i}") for i in range(4)]
        passed = {"DVE": sem("dve_passed"), "Pool": sem("pool_passed"), "SP": sem("sp_passed")}
        pool_cleared, consts_ready, dve_consts = sem("pool_cleared"), sem("consts_ready"), sem("dve_consts")
        bias_step = sem("bias_step")
        lat_made, lat_copied = sem("lat_made"), sem("lat_copied")
        q_made, q_copied, kv_made, kv_copied = sem("q_made"), sem("q_copied"), sem("kv_made"), sem("kv_copied")
        qk_pool, qk_dve, logits_ready = sem("qk_pool"), sem("qk_dve"), sem("logits_ready")
        max_ready, exp_ready = sem("max_ready"), sem("exp_ready")
        inv_ready, probs_ready = sem("inv_ready"), sem("probs_ready")
        pv_pool, pv_dve, oT_made, oT_copied = sem("pv_pool"), sem("pv_dve"), sem("oT_made"), sem("oT_copied")
        attn_made, resid_ready, mean_ready = sem("attn_made"), sem("resid_ready"), sem("mean_ready")
        square_ready, vars_ready, rstds_ready = sem("square_ready"), sem("vars_ready"), sem("rstds_ready")
        x1_ready, score_ready = sem("x1_ready"), sem("score_ready")
        gated_ready, z_ready, zmean_ready = sem("gated_ready"), sem("z_ready"), sem("zmean_ready")
        zsquare_ready = sem("zsquare_ready")
        out_ready = sem("out_ready")
        score_kept, compared, ranked = sem("score_kept"), sem("compared"), sem("ranked")
        rank_added = sem("rank_added")
        rank_step, routed, gate_exped = sem("rank_step"), sem("routed"), sem("gate_exped")
        kept_route, last_route, last_gate, gate_summed = (sem("kept_route"), sem("last_route"), sem("last_gate"),
                                                          sem("gate_summed"))
        chosenT_made, chosenT_copied = sem("chosenT_made"), sem("chosenT_copied")
        hid_made, hid_ready, proc_made, proc_ready = sem("hid_made"), sem("hid_ready"), sem("proc_made"), sem("proc_ready")

        def wait(eng, s, value):
            if not (isinstance(value, int) and value <= 0):
                eng.wait_ge(s, value)

        def wait_alone(eng, s, value):
            wait(eng, s, value)
            if not isinstance(value, int):
                eng.sem_inc(passed[eng.engine.name], 1)

        N_PROJ, N_REST = 5, 6
        N_ZERO = 1 + B * K // (2 * P)
        QK, SM, PV, SUM, OUT, NORM = 1, 2, 3, 4, 5, 6
        LAST = 3 * TB + 4
        FIRST = 5

        def late(t, lag):
            return (t - LAST - lag) % TB

        def late_uses(b, t, lag, ring):
            return (b - 3) * (TB // ring) + (t - LAST % TB - lag) // ring + 1

        def pool_heads(b, t, ago):
            if t < ago:
                b, t = b - 1, t + TB
            first = isinstance(b, int) and b < 2
            return (QH_POOL_FIRST if first else QH_POOL)[t - ago], (PG_POOL_FIRST if first else PG_POOL)[t - ago]

        def has(T, lag):
            return not isinstance(T, int) or 0 <= T - lag < TILES

        def batch(b, lag):
            return not isinstance(b, int) or 0 <= b - lag < B

        def program(eng, step):
            for b in range(FIRST):
                for t in range(TB):
                    step(b, t)
            with eng.Fori(FIRST, B) as b:
                for t in range(TB):
                    step(b, t)
            for b in range(B, B + 4):
                for t in range(TB):
                    step(b, t)

        def hidden_tiles(t):
            return {5: (2, (0, 1)), 6: (2, (2, 3)), 7: (2, (4, 5)), 0: (3, (6, 7))}.get(t, (2, ()))

        def slot_tiles(t):
            return {1: (0,), 2: (1, 2), 3: (3,)}.get(t, ())

        def compared_tiles(t):
            return {6: (1, (0, 1, 2)), 7: (1, (3, 4, 5)), 0: (2, (6, 7))}.get(t, (1, ()))

        def scattered_tiles(t):
            return {2: (0, 1, 2, 3), 3: (4, 5, 6, 7)}.get(t, ())

        block = ctx.enter_context(nc.Block())

        @block.sync
        def _(sp):
            def load_xT(T, t):
                wait_alone(sp, attn_made, T - TB + 1)
                sp.dma_start(xT_sb[:, t % TB, :, :], xT[bass.ds(T * P, P), :].rearrange("k (a n) -> k a n", a=KD)
                             ).then_inc(xT_loaded[t % TB], 16)

            sp.dma_start(wdown_sb[:], Wdown.rearrange("(a k) n -> k a n", a=KD)).then_inc(proj_loaded, 16)
            load_xT(0, 0)
            sp.dma_start(bdown_sb[:], bdown).then_inc(proj_loaded, 16)
            sp.dma_start(wq_sb[:], Wq.rearrange("(a k) n -> k a n", a=KD)).then_inc(proj_loaded, 16)
            sp.dma_start(bias_sb, biases).then_inc(proj_loaded, 16)
            sp.dma_start(wup_sb[:], Wup).then_inc(proj_loaded, 16)
            load_xT(1, 1)
            sp.wait_ge(bias_step, 5)
            for c in range(3):
                sp.dma_start(bias_parts[c:c + 1, :], bias_cut[:, c, :]).then_inc(parts_loaded, 16)
            sp.dma_start(wout_sb[:], Wout.rearrange("(a k) n -> k a n", a=KD)).then_inc(rest_loaded, 16)
            sp.dma_start(router_sb[:], w_router.broadcast_to([P, D])).then_inc(rest_loaded, 16)
            sp.dma_start(b1_sb[:], b1).then_inc(rest_loaded, 16)
            half = F // 2
            for c in range(2):
                sp.dma_start(w1_sb[:, :, c * half:(c + 1) * half],
                             W1[:, c * half:(c + 1) * half].rearrange("(a k) n -> k a n", a=KD)
                             ).then_inc(rest_loaded, 16)
            sp.dma_start(w2_sb[:], W2.rearrange("(a k) n -> k a n", a=FT)).then_inc(rest_loaded, 16)

            def step(b, t):
                T = b * TB + t
                if has(T, LAST):
                    f = T - LAST
                    wait_alone(sp, z_ready, f - 3)
                    sp.dma_start(x1_back[:, t % 4, :], x1_dram[bass.ds(f * P, P), :]
                                 ).then_inc(x1_back_loaded[t % 4], 16)
                if has(T, 0):
                    load_xT(T + 2, t + 2)
                if has(T, LAST + 3):
                    f = T - LAST - 3
                    u = late(t, 3) % 2
                    wait_alone(sp, out_ready, f + 1)
                    sp.dma_start(out[bass.ds(f * P, P), :], out_sb[:, u, :]).then_inc(out_stored[u], 16)
                if has(T, NORM):
                    i = T - NORM
                    c = (t - NORM) % 4
                    wait_alone(sp, x1_ready, i + 1)
                    sp.dma_start(x1_dram[bass.ds(i * P, P), :], x1_sb[:, c, :]).then_inc(x1_stored[c], 16)
                if batch(b, 1) and t == 5:
                    wait_alone(sp, score_kept, b)
                    sp.dma_start(score_dram.rearrange("a (t p) -> (a p) t", p=P), score_old[:],
                                 allow_slow_non_contiguous=True).then_inc(score_stored, 16)
                    wait_alone(sp, score_stored, 16 * b)
                    wait_alone(sp, compared, TB * (b - 1))
                    sp.dma_start(score_row[:], score_dram.broadcast_to([P, S])).then_inc(row_loaded, 16)
                if batch(b, 2) and t == 4:
                    wait_alone(sp, chosen_scattered, 16 * TB * (b - 1))
                    wait_alone(sp, chosenT_made, KD * (b - 2))
                    sp.dma_start(chosen_x[:], chosen_dram.rearrange("(s p) d -> p s d", p=P)
                                 ).then_inc(chosen_loaded, 16)
                if batch(b, 1) and t == 6:
                    for c in range(4):
                        wait_alone(sp, x1_stored[c], 16 * TB // 4 * b)
                    wait_alone(sp, chosen_scattered, 16 * TB * (b - 1))
                    sp.dma_start(x1_batch[:], x1_dram[bass.ds((b - 1) * S, S), :].rearrange("(n p) d -> p n d", p=P)
                                 ).then_inc(batch_loaded, 16)
                if batch(b, 3):
                    if t == 2 and isinstance(b, int) and b == 3:
                        sp.wait_ge(zero_stored, 16 * N_ZERO)
                    for s in {2: (0,), 3: (1, 2, 3)}.get(t, ()):
                        n = (b - 3) * SB_ + s
                        wait_alone(sp, proc_ready, n + 1)
                        sp.dma_start(proc_dram[bass.ds(n * P, P), :], proc_sb[:, s, :]
                                     ).then_inc(proc_stored[s], 16)
                if isinstance(b, int) and b == 0 and t == 0:
                    sp.wait_ge(dve_consts, 1)
                    sp.dma_start(proc_dram[ZROW:ZROW + 1, :], zero_rows[0:1, 0:D]).then_inc(zero_stored, 16)
                    rows = 2 * P
                    for n in range(B * K // rows):
                        sp.dma_start(proc_dram[n * rows:(n + 1) * rows, :].rearrange("(p a) d -> p (a d)", p=P),
                                     zero_rows[:]).then_inc(zero_stored, 16)

            program(sp, step)
            for c in range(2):
                sp.wait_ge(out_stored[c], 16 * TILES // 2)
                sp.wait_ge(xT_loaded[c], 16 * (B + 1))
            for c in range(4):
                sp.wait_ge(x1_stored[c], 16 * TILES // 4)
            for s in range(SB_):
                sp.wait_ge(proc_stored[s], 16 * B)

        @block.tensor
        def _(pe):
            def bias_rows(acc, n):
                pe.matmul(acc[:, 0:D], ones_parts[:], bias_parts[:, n * D:(n + 1) * D], start=True, stop=False)

            def step(b, t):
                T = b * TB + t
                if has(T, 0):
                    wait(pe, xT_loaded[t], 16 * (b + 1))
                    wait(pe, kv_copied, T)
                    for a in range(KD):
                        mm = pe.matmul(psKV[0:L, 0:P], wdown_sb[:, a, :], xT_sb[:, t, a, :],
                                       start=(a == 0), stop=(a == KD - 1))
                    mm.then_inc(lat_made, 1)
                    wait(pe, q_copied, T)
                    if isinstance(T, int) and T == 0:
                        pe.wait_ge(bias_step, 5)
                        for n in range(3):
                            pe.matmul(psQ[:, 0:D], ones_parts[0:1, :], bias_cut[:, n, 0:D], start=(n == 0), stop=False)
                    else:
                        if isinstance(T, int) and T == 1:
                            pe.wait_ge(parts_loaded, 48)
                        bias_rows(psQ, 0)
                    for a in range(KD):
                        mm = pe.matmul(psQ[:, 0:D], xT_sb[:, t, a, :], wq_sb[:, a, :],
                                       start=False, stop=(a == KD - 1))
                    mm.then_inc(q_made, 1)
                if isinstance(T, int) and T == OUT:
                    pe.wait_ge(rest_loaded, 16 * N_REST)
                if has(T, OUT):
                    i = T - OUT
                    wait(pe, resid_ready, i)
                    bias_rows(psW, 1)
                    for a in range(KD):
                        pe.matmul(psW[:, a * P:(a + 1) * P], xT_sb[:, (t - OUT) % TB, a, :], ident[:],
                                  start=False, stop=False)
                    wait(pe, oT_copied, i + 1)
                    for a in range(KD):
                        mm = pe.matmul(psW[:, 0:D], oT_sb[:, a, :], wout_sb[:, a, :],
                                       start=False, stop=(a == KD - 1))
                    mm.then_inc(attn_made, 1)
                if has(T, 0):
                    wait(pe, lat_copied, T + 1)
                    pe.matmul(psKV[:], latT_sb[:], wup_sb[:], start=True, stop=True).then_inc(kv_made, 1)
                if has(T, SUM):
                    i = T - SUM
                    u = (t - SUM) % 2
                    wait(pe, oT_copied, i)
                    _, pool_values = pool_heads(b, t, 1)
                    for g in range(H):
                        if g == 0:
                            wait(pe, pv_pool, i + 1)
                        if g == pool_values:
                            wait(pe, pv_dve, i + 1)
                        for a in range(KD):
                            mm = pe.matmul(psO[a][:, 0:P], pv_prod[:, u, g * D + a * P:g * D + (a + 1) * P], ident[:],
                                           start=(g == 0), stop=(g == H - 1), is_transpose=True)
                    mm.then_inc(oT_made, 1)
                if batch(b, 2) and t == 4:
                    wait(pe, chosen_loaded, 16 * (b - 1))
                    wait(pe, proc_ready, (b - 2) * SB_)
                    for a in range(KD):
                        for s in range(SB_):
                            mm = pe.transpose(psF[a][:, s * P:(s + 1) * P], chosen_x[:, s, a * P:(a + 1) * P], ident[:])
                        mm.then_inc(chosenT_made, 1)
                lag, hidden = hidden_tiles(t)
                if batch(b, lag):
                    for f in hidden:
                        n = (b - lag) * FT + f
                        wait(pe, hid_ready, n - 1)
                        if f < 2:
                            wait(pe, chosenT_copied, KD * (b - 1))
                        for a in range(KD):
                            mm = pe.matmul(psF[f % 2][:], w1_sb[:, a, f * P:(f + 1) * P], chosenT[:, a, :],
                                           start=(a == 0), stop=(a == KD - 1))
                        mm.then_inc(hid_made, 1)
                if batch(b, 3):
                    for s in slot_tiles(t):
                        n = (b - 3) * SB_ + s
                        wait(pe, hid_ready, (b - 2) * FT)
                        wait(pe, proc_ready, n - 1)
                        bias_rows(psF[s % 2], 2)
                        for f in range(FT):
                            mm = pe.matmul(psF[s % 2][:, 0:D], hidT[:, f, s * P:(s + 1) * P], w2_sb[:, f, :],
                                           start=False, stop=(f == FT - 1))
                        mm.then_inc(proc_made, 1)
                lag, tiles = compared_tiles(t)
                if batch(b, lag):
                    for j in tiles:
                        wait(pe, compared, TB * (b - lag) + j + 1)
                        if j == 0:
                            wait(pe, ranked, b - lag)
                        for n in range(TB):
                            mm = pe.matmul(psR[:, n:n + 1], beats[:, j, n * P:(n + 1) * P], ones_col[:],
                                           start=(j == 0 and n == 0), stop=False, skip_group_check=True)
                        mm = pe.matmul(psR[:, j:j + 1], ties[:, j, :], ones_col[:],
                                       start=False, stop=(j == TB - 1), skip_group_check=True)
                        mm.then_inc(rank_added, 1)

            pe.wait_ge(proj_loaded, 16 * N_PROJ)
            pe.wait_ge(consts_ready, 1)
            pe.wait_ge(dve_consts, 1)
            program(pe, step)

        @block.scalar
        def _(act):
            def evacuate_proc(b, slots):
                if batch(b, 3):
                    for s in slots:
                        wait(act, proc_made, (b - 3) * SB_ + s + 1)
                        wait(act, proc_stored[s], 16 * (b - 3))
                        nc.scalar.activation(proc_sb[:, s, :], psF[s % 2][:, 0:D], ACT.Copy).then_inc(proc_ready, 1)

            def step(b, t):
                T = b * TB + t
                if has(T, 0):
                    wait(act, lat_made, T + 1)
                    wait(act, kv_made, T)
                    nc.scalar.activation(latT_sb[0:L, :], psKV[0:L, 0:P], ACT.Identity, bias=bdown_sb[:]
                                         ).then_inc(lat_copied, 1)
                if has(T, LAST + 1):
                    f = T - LAST - 1
                    n = late(t, 1)
                    wait(act, upd_gathered[n % 4], 16 * late_uses(b, t, 1, 4))
                    if n == 0:
                        wait(act, last_gate, b - 2)
                    wait(act, z_ready, f - 1)
                    nc.scalar.activation(upd_gated[:, n % 2, :], upd[:, n % 4, :], ACT.Copy, scale=gate[2][:, n:n + 1]
                                         ).then_inc(gated_ready, 1)
                if has(T, LAST + 2):
                    f = T - LAST - 2
                    wait(act, z_ready, f + 1)
                    z = late(t, 2) % 4
                    wait(act, out_ready, f - 3)
                    nc.scalar.activation(z_neg_mean[:, z:z + 1], z_total[:], ACT.Copy, scale=-1.0 / D
                                         ).then_inc(zmean_ready, 1)
                    wait(act, zmean_ready, f + 1)
                    wait(act, vars_ready, T - OUT)
                    wait(act, zsquare_ready, f)
                    nc.scalar.activation(z_square_junk[:], z_sb[:, z, :], ACT.Square, bias=z_neg_mean[:, z:z + 1],
                                         accum_out=square_sums[:, 1:2]).then_inc(zsquare_ready, 1)
                if has(T, 0):
                    wait(act, q_made, T + 1)
                    wait(act, qk_dve, T - 1)
                    wait(act, qk_pool, T - 1)
                    nc.scalar.activation(q_sb[:, t % 2, :], psQ[:, 0:D], ACT.Copy, scale=SCALE).then_inc(q_copied, 1)
                    wait(act, kv_made, T + 1)
                    wait(act, pv_dve, T - 3)
                    wait(act, pv_pool, T - 3)
                    nc.scalar.activation(kv_sb[:, t % 4, :], psKV[:], ACT.Copy).then_inc(kv_copied, 1)
                evacuate_proc(b, {2: (0,), 3: (1, 2)}.get(t, ()))
                if has(T, OUT):
                    i = T - OUT
                    v = (t - OUT) % 2
                    wait(act, attn_made, i + 1)
                    wait(act, x1_ready, i - 1)
                    wait(act, mean_ready, i)
                    nc.scalar.activation(resid[:, v, :], psW[:, 0:D], ACT.Copy, accum_out=total[:]
                                         ).then_inc(resid_ready, 1)
                    wait(act, resid_ready, i + 1)
                    nc.scalar.activation(neg_mean[:, v:v + 1], total[:], ACT.Copy, scale=-1.0 / D
                                         ).then_inc(mean_ready, 1)
                    wait(act, mean_ready, i + 1)
                    wait(act, vars_ready, T - OUT)
                    wait(act, square_ready, i)
                    nc.scalar.activation(square_junk[:], resid[:, v, :], ACT.Square, bias=neg_mean[:, v:v + 1],
                                         accum_out=square_sums[:, 0:1]).then_inc(square_ready, 1)
                if batch(b, 1) and t == 6:
                    wait(act, score_kept, b)
                    wait(act, gate_summed, b - 1)
                    nc.scalar.activation(gate_exp[:], score_old[:], ACT.Exp, scale=-1.0).then_inc(gate_exped, 1)
                if has(T, SM):
                    i = T - SM
                    u = (t - SM) % 2
                    wait(act, max_ready, i + 1)
                    wait(act, probs_ready, i)
                    for h in range(H):
                        e = nc.scalar.activation(expo[:, h * H:(h + 1) * H], logits[:, u, h * H:(h + 1) * H], ACT.Exp,
                                                 bias=neg_max[:, u, h:h + 1], accum_out=row_sum[:, h:h + 1])
                    e.then_inc(exp_ready, 1)
                if has(T, SUM):
                    i = T - SUM
                    wait(act, oT_made, i + 1)
                    wait(act, attn_made, i)
                    for a in range(KD):
                        o = nc.scalar.activation(oT_sb[:, a, :], psO[a][:, 0:P], ACT.Copy)
                    o.then_inc(oT_copied, 1)
                if batch(b, 2):
                    if t == 4:
                        for a in range(KD):
                            wait(act, chosenT_made, KD * (b - 2) + a + 1)
                            wait(act, hid_made, (b - 2) * FT)
                            nc.scalar.activation(chosenT[:, a, :], psF[a][:], ACT.Copy).then_inc(chosenT_copied, 1)
                lag, hidden = hidden_tiles(t)
                if batch(b, lag):
                    for f in hidden:
                        wait(act, hid_made, (b - lag) * FT + f + 1)
                        wait(act, proc_made, (b - lag) * SB_)
                        nc.scalar.activation(hidT[:, f, :], psF[f % 2][:], ACT.Gelu_apprx_tanh,
                                             bias=b1_sb[:, f:f + 1]).then_inc(hid_ready, 1)
                if t == 3:
                    evacuate_proc(b, (3,))

            act.wait_ge(proj_loaded, 16 * N_PROJ)
            act.wait_ge(dve_consts, 1)
            program(act, step)

        def heads(ap, h0, h1):
            return ap.rearrange("p (h d) -> p h d", h=H)[:, h0:h1, :].unsqueeze(2).broadcast_to([P, h1 - h0, H, DH])

        def qk_products(eng, t, h0, h1):
            u = t % 2
            keys = kv_sb[:, t % 4, :].rearrange("p (g e) -> p g e", g=H)[:, :, 0:DH]
            return eng.tensor_tensor(
                qk_prod[:, u, h0 * H * DH:h1 * H * DH].rearrange("p (h g d) -> p h g d", h=h1 - h0, g=H),
                heads(q_sb[:, u, :], h0, h1), keys.unsqueeze(1).broadcast_to([P, h1 - h0, H, DH]), ALU.mult)

        def pv_products(eng, t, g0, g1):
            u = t % 2
            weight = probs[:, u, :].rearrange("p (h g) -> p g h", h=H)[:, g0:g1, :]
            values = kv_sb[:, t % 4, :].rearrange("p (g e) -> p g e", g=H)[:, g0:g1, DH:2 * DH]
            return eng.tensor_tensor(
                pv_prod[:, u, g0 * H * DH:g1 * H * DH].rearrange("p (g h d) -> p g h d", g=g1 - g0, h=H),
                weight.unsqueeze(3).broadcast_to([P, g1 - g0, H, DH]),
                values.unsqueeze(2).broadcast_to([P, g1 - g0, H, DH]), ALU.mult)

        @block.gpsimd
        def _(pool):
            pool.memset(ident[:], 0.0).then_inc(pool_cleared, 1)
            pool.memset(after[:], 1.0).then_inc(pool_cleared, 1)
            pool.wait_ge(pool_cleared, 2)
            pool.affine_select(out=ident[:], in_=ident[:], compare_op=ALU.not_equal, fill=1.0, base=0,
                               pattern=[[-1, P]], channel_multiplier=1).then_inc(pool_cleared, 1)
            pool.affine_select(out=after[:], in_=after[:], compare_op=ALU.is_gt, fill=0.0, base=0,
                               pattern=[[1, P]], channel_multiplier=-1).then_inc(pool_cleared, 1)
            pool.wait_ge(pool_cleared, 4)
            pool.memset(minus_half[:], -0.5).then_inc(consts_ready, 1)
            pool.wait_ge(dve_consts, 1)
            pool.wait_ge(consts_ready, 1)

            def gather_update(b, t):
                T = b * TB + t
                if has(T, LAST):
                    f = T - LAST
                    n = late(t, 0)
                    if n == 0:
                        for s in range(SB_):
                            wait(pool, proc_stored[s], 16 * (b - 2))
                        wait(pool, zero_stored, 16 * N_ZERO)
                        wait(pool, last_route, b - 2)
                    wait_alone(pool, gated_ready, f - 3)
                    pool.indirect_dma_start(upd[:, n % 4, :], None, proc_dram,
                                            bass.IndirectOffsetOnAxis(route[2][:, n:n + 1], 0)
                                            ).then_inc(upd_gathered[n % 4], 16)

            def step(b, t):
                T = b * TB + t
                last_batch = isinstance(T, int) and T - LAST >= TILES - TB
                if last_batch:
                    gather_update(b, t)
                if has(T, NORM) or has(T, LAST + 3):
                    wait(pool, vars_ready, T - NORM + 1)
                    if has(T - 1, NORM):
                        wait(pool, x1_ready, T - NORM)
                    if has(T - 1, LAST + 3):
                        wait(pool, out_ready, T - LAST - 3)
                    pool.tensor_tensor(rstds[:], vars_eps[:], minus_half[:], ALU.pow).then_inc(rstds_ready, 1)
                if has(T, QK):
                    i = T - QK
                    wait(pool, q_copied, i + 1)
                    wait(pool, kv_copied, i + 1)
                    wait(pool, logits_ready, 2 * (i - 1))
                    qk_products(pool, t - QK, 0, pool_heads(b, t, 0)[0]).then_inc(qk_pool, 1)
                if not last_batch:
                    gather_update(b, t)
                if has(T, PV):
                    i = T - PV
                    wait(pool, probs_ready, i + 1)
                    wait(pool, oT_made, i - 1)
                    pv_products(pool, t - PV, 0, pool_heads(b, t, 0)[1]).then_inc(pv_pool, 1)
                if batch(b, 2) and scattered_tiles(t):
                    if t == 2:
                        wait(pool, routed, b - 1)
                        wait(pool, batch_loaded, 16 * (b - 1))
                        wait_alone(pool, chosen_loaded, 16 * (b - 2))
                    for n in scattered_tiles(t):
                        pool.indirect_dma_start(chosen_dram, bass.IndirectOffsetOnAxis(rank_u[:, n:n + 1], 0),
                                                x1_batch[:, n, :], None, bounds_check=K - 1, oob_is_err=False
                                                ).then_inc(chosen_scattered, 16)

            program(pool, step)

        @block.vector
        def _(dve):
            dve.memset(latT_sb[L:L + 1, :], 1.0)
            dve.memset(ones_parts[:], 1.0)
            dve.memset(ones_col[:], 1.0)
            dve.memset(slot_base[:], float(-ZROW))
            dve.memset(square_sums[:], 0.0)
            dve.memset(zero_rows[:], 0.0).then_inc(dve_consts, 1)
            dve.wait_ge(proj_loaded, 16 * N_PROJ)
            dve.tensor_copy(bias_cut[:, 0, :], bias_sb).then_inc(bias_step, 1)
            dve.wait_ge(bias_step, 1)
            dve.tensor_tensor(bias_rest, bias_sb, bias_cut[:, 0, :], ALU.subtract).then_inc(bias_step, 1)
            dve.wait_ge(bias_step, 2)
            dve.tensor_copy(bias_cut[:, 1, :], bias_rest).then_inc(bias_step, 1)
            dve.wait_ge(bias_step, 3)
            dve.tensor_tensor(bias_rest, bias_rest, bias_cut[:, 1, :], ALU.subtract).then_inc(bias_step, 1)
            dve.wait_ge(bias_step, 4)
            dve.tensor_copy(bias_cut[:, 2, :], bias_rest).then_inc(bias_step, 1)
            dve.wait_ge(consts_ready, 1)

            def reduce_logits(u, h0, h1):
                return dve.tensor_reduce(
                    logits[:, u, h0 * H:h1 * H],
                    qk_prod[:, u, h0 * H * DH:h1 * H * DH].rearrange("p (n d) -> p n d", d=DH), AX.X, ALU.add)

            def compare_scores(b, t):
                lag, tiles = compared_tiles(t)
                if batch(b, lag):
                    if t == 6:
                        wait(dve, row_loaded, 16 * b)
                    for j in tiles:
                        own = score_old[:, j:j + 1]
                        wait(dve, rank_added, TB * (b - lag - 1) + j + 1)
                        dve.tensor_scalar(beats[:, j, 0:(j + 1) * P], score_row[:, 0:(j + 1) * P], own, None,
                                          ALU.is_lt)
                        if j < TB - 1:
                            dve.tensor_scalar(beats[:, j, (j + 1) * P:S], score_row[:, (j + 1) * P:S], own, None,
                                              ALU.is_le)
                        dve.scalar_tensor_tensor(out=ties[:, j, :], in0=score_row[:, j * P:(j + 1) * P], scalar=own,
                                                 in1=after[:], op0=ALU.is_equal, op1=ALU.mult).then_inc(compared, 1)

            def step(b, t):
                T = b * TB + t
                if batch(b, 3) and t == 4:
                    for c in range(4):
                        wait(dve, upd_gathered[c], (b - 3) * (16 * TB // 4))
                    wait(dve, kept_route, b - 2)
                    dve.tensor_copy(route[2][:], route[1][:]).then_inc(last_route, 1)
                if has(T, SM):
                    i = T - SM
                    wait(dve, exp_ready, i - 1)
                    wait(dve, qk_dve, i + 1)
                    pool_queries, _ = pool_heads(b, t, 1)
                    reduce_logits((t - SM) % 2, pool_queries, H).then_inc(logits_ready, 1)
                    wait(dve, qk_pool, i + 1)
                    reduce_logits((t - SM) % 2, 0, pool_queries).then_inc(logits_ready, 1)
                if not has(T, QK):
                    compare_scores(b, t)
                if has(T, NORM):
                    i = T - NORM
                    c = (t - NORM) % 4
                    if isinstance(T, int) and T == NORM:
                        dve.wait_ge(rest_loaded, 16 * N_REST)
                    wait(dve, rstds_ready, i + 1)
                    wait(dve, x1_stored[c], 16 * (2 * b + (t - NORM) // 4))
                    v = (t - NORM) % 2
                    dve.tensor_scalar(x1_sb[:, c, :], resid[:, v, :], neg_mean[:, v:v + 1], rstds[:, 0:1],
                                      ALU.add, ALU.mult).then_inc(x1_ready, 1)
                if has(T, LAST + 3):
                    f = T - LAST - 3
                    u = late(t, 3) % 2
                    z = late(t, 3) % 4
                    wait(dve, rstds_ready, T - NORM + 1)
                    wait(dve, out_stored[u], 16 * (late_uses(b, t, 3, 2) - 1))
                    dve.tensor_scalar(out_sb[:, u, :], z_sb[:, z, :], z_neg_mean[:, z:z + 1],
                                      rstds[:, 1:2], ALU.add, ALU.mult).then_inc(out_ready, 1)
                if has(T, SM):
                    wait(dve, logits_ready, 2 * (T - SM + 1))
                    dve.tensor_reduce(neg_max[:, (t - SM) % 2, :], logits[:, (t - SM) % 2, :].rearrange("p (h g) -> p h g", h=H), AX.X, ALU.max,
                                      negate=True).then_inc(max_ready, 1)
                if has(T, NORM):
                    i = T - NORM
                    c = (t - NORM) % 4
                    wait(dve, x1_ready, i + 1)
                    wait(dve, score_ready, i)
                    if t == NORM:
                        wait(dve, score_kept, b)
                    n = (t - NORM) % TB
                    dve.tensor_tensor_reduce(out=score_junk[:], in0=x1_sb[:, c, :], in1=router_sb[:], scale=1.0,
                                             scalar=0.0, op0=ALU.mult, op1=ALU.add,
                                             accum_out=score_new[:, n:n + 1]).then_inc(score_ready, 1)
                if batch(b, 1) and t == 5:
                    wait(dve, score_ready, TB * b)
                    wait(dve, score_stored, 16 * (b - 1))
                    wait(dve, gate_exped, b - 1)
                    wait(dve, compared, TB * (b - 1))
                    dve.tensor_copy(score_old[:], score_new[:]).then_inc(score_kept, 1)
                if has(T, PV):
                    i = T - PV
                    wait(dve, exp_ready, i + 1)
                    dve.reciprocal(row_inv[:], row_sum[:]).then_inc(inv_ready, 1)
                if has(T, LAST + 1):
                    f = T - LAST - 1
                    u = late(t, 1) % 2
                    z = late(t, 1) % 4
                    wait(dve, gated_ready, f + 1)
                    wait(dve, x1_back_loaded[z], 16 * late_uses(b, t, 1, 4))
                    wait(dve, out_ready, f - 3)
                    wait(dve, zmean_ready, f)
                    dve.scalar_tensor_tensor(out=z_sb[:, z, :], in0=x1_back[:, z, :], scalar=2.0,
                                             in1=upd_gated[:, u, :],
                                             op0=ALU.mult, op1=ALU.add, accum_out=z_total[:]).then_inc(z_ready, 1)
                if has(T, PV):
                    wait(dve, inv_ready, i + 1)
                    wait(dve, pv_pool, i - 1)
                    wait(dve, pv_dve, i - 1)
                    dve.tensor_tensor(probs[:, (t - PV) % 2, :].rearrange("p (h g) -> p h g", h=H),
                                      expo[:].rearrange("p (h g) -> p h g", h=H),
                                      row_inv[:].unsqueeze(2).broadcast_to([P, H, H]), ALU.mult
                                      ).then_inc(probs_ready, 1)
                if has(T, QK):
                    i = T - QK
                    wait(dve, q_copied, i + 1)
                    wait(dve, kv_copied, i + 1)
                    wait(dve, logits_ready, 2 * (i - 1))
                    qk_products(dve, t - QK, pool_heads(b, t, 0)[0], H).then_inc(qk_dve, 1)
                if has(T, PV):
                    i = T - PV
                    wait(dve, probs_ready, i + 1)
                    wait(dve, oT_made, i - 1)
                    pv_products(dve, t - PV, pool_heads(b, t, 0)[1], H).then_inc(pv_dve, 1)
                if has(T, QK):
                    compare_scores(b, t)
                if batch(b, 3) and t == 1:
                    wait(dve, last_route, b - 3)
                    wait(dve, last_gate, b - 3)
                    dve.tensor_copy(gate[1][:], gate[0][:])
                    dve.tensor_copy(route[1][:], route[0][:]).then_inc(kept_route, 1)
                if batch(b, 2) and t == 1:
                    r = 3 * (b - 2)
                    wait(dve, rank_added, TB * (b - 1))
                    wait(dve, chosen_scattered, 16 * TB * (b - 2))
                    dve.tensor_copy(rank_f[:], psR[:, 0:TB]).then_inc(ranked, 1)
                    wait(dve, gate_exped, b - 1)
                    dve.tensor_scalar(gate_sum[:], gate_exp[:], 1.0, None, ALU.add).then_inc(gate_summed, 1)
                    wait(dve, ranked, b - 1)
                    dve.tensor_scalar(chosen[:], rank_f[:], float(K), None, ALU.is_lt)
                    dve.tensor_scalar(route_f[:], rank_f[:], slot_base[:], None, ALU.add).then_inc(rank_step, 1)
                    dve.tensor_copy(rank_u[:], rank_f[:])
                    dve.tensor_scalar(slot_base[:], slot_base[:], float(K), None, ALU.add)
                    wait(dve, rank_step, r + 1)
                    dve.tensor_tensor(route_f[:], route_f[:], chosen[:], ALU.mult).then_inc(rank_step, 1)
                    wait(dve, gate_summed, b - 1)
                    wait(dve, kept_route, b - 2)
                    dve.reciprocal(gate[0][:], gate_sum[:])
                    wait(dve, rank_step, r + 2)
                    dve.tensor_scalar(route[0][:], route_f[:], float(ZROW), None, ALU.add).then_inc(rank_step, 1)
                    wait(dve, rank_step, r + 3)
                    dve.tensor_copy(rank_f[:], route_f[:]).then_inc(routed, 1)
                if has(T, OUT) or has(T, LAST + 2):
                    if has(T, OUT):
                        wait(dve, square_ready, T - OUT + 1)
                    if has(T, LAST + 2):
                        wait(dve, zsquare_ready, T - LAST - 1)
                    wait(dve, rstds_ready, T - OUT)
                    dve.tensor_scalar(vars_eps[:], square_sums[:], 1.0 / D, EPS, ALU.mult, ALU.add
                                      ).then_inc(vars_ready, 1)
                if batch(b, 3) and t == 4:
                    wait(dve, gated_ready, (b - 3) * TB)
                    dve.tensor_copy(gate[2][:], gate[1][:]).then_inc(last_gate, 1)

            program(dve, step)


_WEIGHTS = ["Wq", "Wdown", "bdown", "Wup", "Wout", "biases", "w_router", "W1", "b1", "W2"]


def kernel(L0_attn_x, L0_attn_Wq, L0_attn_bq, L0_attn_Wdown, L0_attn_bdown, L0_attn_Wup, L0_attn_bup, L0_attn_Wout,
           L0_attn_bout, L0_ffn_w_router, L0_ffn_W1, L0_ffn_b1, L0_ffn_W2, L0_ffn_b2):
    import numpy as np
    import concourse.bacc as bacc
    from concourse.bass_utils import run_bass_kernel_spmd

    Bn, Sn, Dn = L0_attn_x.shape
    x = np.asarray(L0_attn_x).reshape(Bn * Sn, Dn)
    xT = x.reshape(Bn * Sn // P, P, Dn // P, P).transpose(0, 3, 2, 1).reshape(Bn * Sn, Dn)
    pad = np.zeros((2 * P, Dn), x.dtype)
    arrays = {
        "xT": np.concatenate([xT, pad]), "Wq": L0_attn_Wq, "Wdown": L0_attn_Wdown,
        "biases": np.concatenate([np.asarray(v) for v in (L0_attn_bq, L0_attn_bout, L0_ffn_b2)])[None, :],
        "bdown": np.asarray(L0_attn_bdown)[:, None],
        "Wup": np.concatenate([np.asarray(L0_attn_Wup), np.asarray(L0_attn_bup)[None, :]]),
        "Wout": L0_attn_Wout, "w_router": np.asarray(L0_ffn_w_router)[None, :],
        "W1": L0_ffn_W1, "b1": np.asarray(L0_ffn_b1).reshape(-1, P).T, "W2": L0_ffn_W2,
    }
    arrays = {k: np.ascontiguousarray(v) for k, v in arrays.items()}
    nc = bacc.Bacc("TRN2", target_bir_lowering=False, num_devices=1)
    ap = {k: nc.dram_tensor(k, v.shape, mybir.dt.from_np(v.dtype), kind="ExternalInput").ap()
          for k, v in arrays.items()}
    out = nc.dram_tensor("out", (Bn * Sn, Dn), F32, kind="ExternalOutput").ap()
    x1_dram = nc.dram_tensor("x1_dram", (Bn * Sn, Dn), F32, kind="Internal").ap()
    score_dram = nc.dram_tensor("score_dram", (1, Sn), F32, kind="Internal").ap()
    chosen_dram = nc.dram_tensor("chosen_dram", (Sn // 2, Dn), F32, kind="Internal").ap()
    proc_dram = nc.dram_tensor("proc_dram", (Bn * Sn // 2 + 1, Dn), F32, kind="Internal").ap()
    build_layer(nc, ap["xT"], *[ap[k] for k in _WEIGHTS], out, x1_dram, score_dram, chosen_dram, proc_dram)
    r = run_bass_kernel_spmd(nc, [arrays], core_ids=[0])
    return r.results[0]["out"].reshape(Bn, Sn, Dn)
```
